# Optimizing a Trainium2 kernel written in Bass

```python
import numpy as np
import jax
import jax.numpy as jnp

def _softmax(x, axis=-1):
    return jax.nn.softmax(x, axis=axis)

def _gelu(x):
    return jax.nn.gelu(x, approximate=True)

def _silu(x):
    return jax.nn.silu(x)

def _sigmoid(x):
    return jax.nn.sigmoid(x)

def _layernorm(x, axis=-1, eps=1e-05):
    m = jnp.mean(x, axis=axis, keepdims=True)
    v = jnp.var(x, axis=axis, keepdims=True)
    return (x - m) / jnp.sqrt(v + eps)

def _scatter_add(tgt, idx, src, axis=0):
    return tgt.at[idx].add(src)

def _segment_sum(src, seg, n):
    return jax.ops.segment_sum(src, seg, n)
kernel_name = 'mk_xattn_ffn_d2_seqx_r8_13cb7c'

def setup_inputs(seed: int=0):
    np.random.seed(seed)
    _w = jnp.asarray

    def _rec_inputs():
        import jax
        import jax.numpy as jnp
        _rk = jax.random.key(seed)
        x = 7.22e-05 + 1 * jax.random.normal(jax.random.fold_in(_rk, 1), (16, 128, 256), jnp.float32)
        _lenS = 128 - jax.random.randint(jax.random.fold_in(_rk, 7), (16,), 0, max(1, 128 // 4) + 1, jnp.int32)
        _lenS2 = 128 - jax.random.randint(jax.random.fold_in(_rk, 8), (16,), 0, max(1, 128 // 4) + 1, jnp.int32)
        _ctx_2048P = jax.random.normal(jax.random.fold_in(_rk, 11), (16, 16, 256), jnp.float32)
        _ctx_2048c = jax.random.dirichlet(jax.random.fold_in(_rk, 511), 0.3 * jnp.ones((16,), jnp.float32), (16, 128))
        _ctx_2048t = jnp.einsum('bsk,bkd->bsd', _ctx_2048c, _ctx_2048P)
        _ctx_2048t = _ctx_2048t * jax.lax.rsqrt(jnp.mean(jnp.square(_ctx_2048t)) + 1e-12) * 0.953939
        ctx_2048 = 4.13588e-05 + 0.999923 * (_ctx_2048t + 0.3 * jax.random.normal(jax.random.fold_in(_rk, 611), (16, 128, 256), jnp.float32))
        return (x, ctx_2048)
    x, ctx_2048 = _rec_inputs()

    def _L0_xattn_setup():
        import jax, jax.numpy as jnp
        import numpy as np
        B, S, DIM, HD = (4, 128, 256, 128)
        H = DIM // HD
        GN_EPS = 0.001

        def _decay_masks(n_heads, seq_len):
            gam = 1.0 - 2.0 ** (-5.0 - jnp.arange(n_heads, dtype=jnp.float32))
            idx = jnp.arange(seq_len, dtype=jnp.float32)
            expo = idx[None, :] - idx[:, None]
            D = jnp.where(expo[None, :, :] <= 0, gam[:, None, None] ** expo[None, :, :], 0.0)
            return D / jnp.sqrt(D.sum(axis=-1))[:, None, :]
        key = jax.random.key(seed)
        ks = jax.random.split(key, 8)
        x = jax.random.normal(ks[0], (B, S, DIM), dtype=jnp.float32)
        k = jax.random.normal(ks[1], (B, S, DIM), dtype=jnp.float32)
        v = jax.random.normal(ks[2], (B, S, DIM), dtype=jnp.float32)
        Wh = jax.random.normal(ks[3], (H, HD, HD), dtype=jnp.float32) / np.sqrt(HD)
        wg_w = jax.random.normal(ks[4], (DIM, DIM), dtype=jnp.float32) / np.sqrt(DIM)
        wo_w = jax.random.normal(ks[5], (DIM, DIM), dtype=jnp.float32) / np.sqrt(DIM)
        gn_gamma = jnp.ones((DIM,), dtype=jnp.float32)
        gn_beta = jnp.zeros((DIM,), dtype=jnp.float32)
        return {'x': x, 'k': k, 'v': v, 'Wh': Wh, 'wg_w': wg_w, 'wo_w': wo_w, 'gn_gamma': gn_gamma, 'gn_beta': gn_beta}
    _L0_xattn_all = _L0_xattn_setup()
    _L0_xattn_in = {k: v for k, v in _L0_xattn_all.items() if k in ('Wh', 'wg_w', 'wo_w', 'gn_gamma', 'gn_beta')}
    del _L0_xattn_all

    def _L0_ffn_setup():
        import jax, jax.numpy as jnp
        import numpy as np
        D_MODEL = 256
        D_FF = 1024
        N_EXPERTS = 4
        B, S = (2, 256)
        key = jax.random.key(seed)
        ks = jax.random.split(key, 6)
        scale = 0.02
        return {'hidden_states': jax.random.normal(ks[0], (B, S, D_MODEL), dtype=jnp.float32), 'Wr': jax.random.normal(ks[1], (D_MODEL, N_EXPERTS), dtype=jnp.float32) * scale, 'br': jnp.zeros((N_EXPERTS,), dtype=jnp.float32), 'Wg': jax.random.normal(ks[2], (N_EXPERTS, D_MODEL, D_FF), dtype=jnp.float32) * scale, 'Wu': jax.random.normal(ks[3], (N_EXPERTS, D_MODEL, D_FF), dtype=jnp.float32) * scale, 'Wd': jax.random.normal(ks[4], (N_EXPERTS, D_FF, D_MODEL), dtype=jnp.float32) * scale}
    _L0_ffn_all = _L0_ffn_setup()
    _L0_ffn_in = {k: v for k, v in _L0_ffn_all.items() if k in ('Wr', 'br', 'Wg', 'Wu', 'Wd')}
    del _L0_ffn_all

    def _L1_xattn_setup():
        import jax, jax.numpy as jnp
        import numpy as np
        DIM = 256
        N_HEADS = 16
        HEAD_DIM = DIM // N_HEADS
        EPS = 1e-06
        IMG_LEN = 257

        def rms_norm(x, g, eps=EPS):
            var = jnp.mean(x * x, axis=-1, keepdims=True)
            return x * jax.lax.rsqrt(var + eps) * g

        def _attend(q, k, v, k_mask=None):
            scale = 1.0 / jnp.sqrt(jnp.asarray(HEAD_DIM, q.dtype))
            scores = jnp.einsum('bqnd,bknd->bnqk', q, k) * scale
            if k_mask is not None:
                neg = jnp.asarray(jnp.finfo(scores.dtype).min, scores.dtype)
                scores = jnp.where(k_mask[:, None, None, :], scores, neg)
            probs = jax.nn.softmax(scores, axis=-1)
            return jnp.einsum('bnqk,bknd->bqnd', probs, v)
        key = jax.random.key(seed)
        ks = jax.random.split(key, 16)
        B, L1, L2 = (1, 2048, 769)
        std = 0.02
        inp = {'x': jax.random.normal(ks[0], (B, L1, DIM), jnp.float32), 'context': jax.random.normal(ks[1], (B, L2, DIM), jnp.float32), 'context_lens': jax.random.randint(ks[2], (B,), 32, 513, jnp.int32), 'Wq': jax.random.normal(ks[3], (DIM, DIM), jnp.float32) * std, 'bq': jnp.zeros((DIM,), jnp.float32), 'gq': jnp.ones((DIM,), jnp.float32), 'Wk': jax.random.normal(ks[4], (DIM, DIM), jnp.float32) * std, 'bk': jnp.zeros((DIM,), jnp.float32), 'gk': jnp.ones((DIM,), jnp.float32), 'Wv': jax.random.normal(ks[5], (DIM, DIM), jnp.float32) * std, 'bv': jnp.zeros((DIM,), jnp.float32), 'Wk_img': jax.random.normal(ks[6], (DIM, DIM), jnp.float32) * std, 'bk_img': jnp.zeros((DIM,), jnp.float32), 'gk_img': jnp.ones((DIM,), jnp.float32), 'Wv_img': jax.random.normal(ks[7], (DIM, DIM), jnp.float32) * std, 'bv_img': jnp.zeros((DIM,), jnp.float32), 'Wo': jax.random.normal(ks[8], (DIM, DIM), jnp.float32) * std, 'bo': jnp.zeros((DIM,), jnp.float32)}
        return inp
    _L1_xattn_all = _L1_xattn_setup()
    _L1_xattn_in = {k: v for k, v in _L1_xattn_all.items() if k in ('context_lens', 'Wq', 'bq', 'gq', 'Wk', 'bk', 'gk', 'Wv', 'bv', 'Wk_img', 'bk_img', 'gk_img', 'Wv_img', 'bv_img', 'Wo', 'bo')}
    del _L1_xattn_all

    def _L1_ffn_setup():
        import jax, jax.numpy as jnp
        import numpy as np
        ALPHA = 1.702
        LIMIT = 7.0
        TOP_K = 4
        B, S, H = (1, 128, 256)
        E, D = (16, 256)
        key = jax.random.key(seed)
        ks = jax.random.split(key, 7)
        s = 0.02
        return {'hidden_states': jax.random.normal(ks[0], (B, S, H), dtype=jnp.float32), 'router_weight': jax.random.normal(ks[1], (E, H), dtype=jnp.float32) * s, 'router_bias': jax.random.normal(ks[2], (E,), dtype=jnp.float32) * s, 'gate_up_proj': jax.random.normal(ks[3], (E, H, 2 * D), dtype=jnp.float32) * s, 'gate_up_proj_bias': jax.random.normal(ks[4], (E, 2 * D), dtype=jnp.float32) * s, 'down_proj': jax.random.normal(ks[5], (E, D, H), dtype=jnp.float32) * s, 'down_proj_bias': jax.random.normal(ks[6], (E, H), dtype=jnp.float32) * s}
    _L1_ffn_all = _L1_ffn_setup()
    _L1_ffn_in = {k: v for k, v in _L1_ffn_all.items() if k in ('router_weight', 'router_bias', 'gate_up_proj', 'gate_up_proj_bias', 'down_proj', 'down_proj_bias')}
    del _L1_ffn_all
    return {'x': x, 'ctx_2048': ctx_2048, 'L0_xattn_Wh': _L0_xattn_in['Wh'], 'L0_xattn_wg_w': _L0_xattn_in['wg_w'], 'L0_xattn_wo_w': _L0_xattn_in['wo_w'], 'L0_xattn_gn_gamma': _L0_xattn_in['gn_gamma'], 'L0_xattn_gn_beta': _L0_xattn_in['gn_beta'], 'L0_ffn_Wr': _L0_ffn_in['Wr'], 'L0_ffn_br': _L0_ffn_in['br'], 'L0_ffn_Wg': _L0_ffn_in['Wg'], 'L0_ffn_Wu': _L0_ffn_in['Wu'], 'L0_ffn_Wd': _L0_ffn_in['Wd'], 'L1_xattn_context_lens': _L1_xattn_in['context_lens'], 'L1_xattn_Wq': _L1_xattn_in['Wq'], 'L1_xattn_bq': _L1_xattn_in['bq'], 'L1_xattn_gq': _L1_xattn_in['gq'], 'L1_xattn_Wk': _L1_xattn_in['Wk'], 'L1_xattn_bk': _L1_xattn_in['bk'], 'L1_xattn_gk': _L1_xattn_in['gk'], 'L1_xattn_Wv': _L1_xattn_in['Wv'], 'L1_xattn_bv': _L1_xattn_in['bv'], 'L1_xattn_Wk_img': _L1_xattn_in['Wk_img'], 'L1_xattn_bk_img': _L1_xattn_in['bk_img'], 'L1_xattn_gk_img': _L1_xattn_in['gk_img'], 'L1_xattn_Wv_img': _L1_xattn_in['Wv_img'], 'L1_xattn_bv_img': _L1_xattn_in['bv_img'], 'L1_xattn_Wo': _L1_xattn_in['Wo'], 'L1_xattn_bo': _L1_xattn_in['bo'], 'L1_ffn_router_weight': _L1_ffn_in['router_weight'], 'L1_ffn_router_bias': _L1_ffn_in['router_bias'], 'L1_ffn_gate_up_proj': _L1_ffn_in['gate_up_proj'], 'L1_ffn_gate_up_proj_bias': _L1_ffn_in['gate_up_proj_bias'], 'L1_ffn_down_proj': _L1_ffn_in['down_proj'], 'L1_ffn_down_proj_bias': _L1_ffn_in['down_proj_bias']}

def reference(x, ctx_2048, L0_xattn_Wh, L0_xattn_wg_w, L0_xattn_wo_w, L0_xattn_gn_gamma, L0_xattn_gn_beta, L0_ffn_Wr, L0_ffn_br, L0_ffn_Wg, L0_ffn_Wu, L0_ffn_Wd, L1_xattn_context_lens, L1_xattn_Wq, L1_xattn_bq, L1_xattn_gq, L1_xattn_Wk, L1_xattn_bk, L1_xattn_gk, L1_xattn_Wv, L1_xattn_bv, L1_xattn_Wk_img, L1_xattn_bk_img, L1_xattn_gk_img, L1_xattn_Wv_img, L1_xattn_bv_img, L1_xattn_Wo, L1_xattn_bo, L1_ffn_router_weight, L1_ffn_router_bias, L1_ffn_gate_up_proj, L1_ffn_gate_up_proj_bias, L1_ffn_down_proj, L1_ffn_down_proj_bias):
    import jax
    import jax.numpy as jnp

    def _L0_xattn_ref(x, k, v, Wh, wg_w, wo_w, gn_gamma, gn_beta):
        import jax, jax.numpy as jnp
        import numpy as np
        B, S, DIM, HD = (4, 128, 256, 128)
        H = DIM // HD
        GN_EPS = 0.001

        def _decay_masks(n_heads, seq_len):
            gam = 1.0 - 2.0 ** (-5.0 - jnp.arange(n_heads, dtype=jnp.float32))
            idx = jnp.arange(seq_len, dtype=jnp.float32)
            expo = idx[None, :] - idx[:, None]
            D = jnp.where(expo[None, :, :] <= 0, gam[:, None, None] ** expo[None, :, :], 0.0)
            return D / jnp.sqrt(D.sum(axis=-1))[:, None, :]
        b, s, dim = x.shape
        h, hd, _ = Wh.shape
        xh = x.reshape(b, s, h, hd)
        kh = k.reshape(b, s, h, hd)
        vh = v.reshape(b, s, h, hd)
        Q = jnp.einsum('bshd,hde->bshe', xh, Wh)
        K = jnp.einsum('bshd,hde->bshe', kh, Wh)
        V = jnp.einsum('bshd,hde->bshe', vh, Wh)
        scores = jnp.einsum('bshe,bthe->bhst', Q, K) / jnp.sqrt(jnp.float32(hd))
        Dn = _decay_masks(h, s)
        masked = scores * Dn[None, :, :, :]
        A = jnp.maximum(jnp.abs(masked.sum(axis=0)), 1.0)
        O = jnp.einsum('hst,bthe->bshe', A, V).reshape(b, s, dim)
        mu = O.mean(axis=-1, keepdims=True)
        var = O.var(axis=-1, keepdims=True)
        Y = (O - mu) / jnp.sqrt(var + GN_EPS) * gn_gamma + gn_beta
        W = jax.nn.relu(x @ wg_w)
        return W * Y @ wo_w

    def _L0_ffn_ref(hidden_states, Wr, br, Wg, Wu, Wd):
        import jax, jax.numpy as jnp
        import numpy as np
        D_MODEL = 256
        D_FF = 1024
        N_EXPERTS = 4
        B, S = (2, 256)
        b, s, d = hidden_states.shape
        x = hidden_states.reshape(-1, d)
        logits = x @ Wr + br
        probs = jax.nn.softmax(logits, axis=-1)
        top_w, top_idx = jax.lax.top_k(probs, 1)
        g = jnp.einsum('td,edf->tef', x, Wg)
        u = jnp.einsum('td,edf->tef', x, Wu)
        h = jax.nn.silu(g) * u
        y = jnp.einsum('tef,efd->ted', h, Wd)
        sel = jnp.take_along_axis(y, top_idx[:, :, None], axis=1)[:, 0]
        out = sel * top_w
        return out.reshape(b, s, d)

    def _L1_xattn_ref(x, context, context_lens, Wq, bq, gq, Wk, bk, gk, Wv, bv, Wk_img, bk_img, gk_img, Wv_img, bv_img, Wo, bo):
        import jax, jax.numpy as jnp
        import numpy as np
        DIM = 256
        N_HEADS = 16
        HEAD_DIM = DIM // N_HEADS
        EPS = 1e-06
        IMG_LEN = 257

        def rms_norm(x, g, eps=EPS):
            var = jnp.mean(x * x, axis=-1, keepdims=True)
            return x * jax.lax.rsqrt(var + eps) * g

        def _attend(q, k, v, k_mask=None):
            scale = 1.0 / jnp.sqrt(jnp.asarray(HEAD_DIM, q.dtype))
            scores = jnp.einsum('bqnd,bknd->bnqk', q, k) * scale
            if k_mask is not None:
                neg = jnp.asarray(jnp.finfo(scores.dtype).min, scores.dtype)
                scores = jnp.where(k_mask[:, None, None, :], scores, neg)
            probs = jax.nn.softmax(scores, axis=-1)
            return jnp.einsum('bnqk,bknd->bqnd', probs, v)
        b = x.shape[0]
        n, d = (N_HEADS, HEAD_DIM)
        ctx_img = context[:, :IMG_LEN]
        ctx_txt = context[:, IMG_LEN:]
        q = rms_norm(x @ Wq + bq, gq).reshape(b, -1, n, d)
        k = rms_norm(ctx_txt @ Wk + bk, gk).reshape(b, -1, n, d)
        v = (ctx_txt @ Wv + bv).reshape(b, -1, n, d)
        k_img = rms_norm(ctx_img @ Wk_img + bk_img, gk_img).reshape(b, -1, n, d)
        v_img = (ctx_img @ Wv_img + bv_img).reshape(b, -1, n, d)
        img_x = _attend(q, k_img, v_img)
        k_mask = jnp.arange(k.shape[1])[None, :] < context_lens[:, None]
        txt_x = _attend(q, k, v, k_mask)
        out = (txt_x + img_x).reshape(b, -1, n * d)
        return out @ Wo + bo

    def _L1_ffn_ref(hidden_states, router_weight, router_bias, gate_up_proj, gate_up_proj_bias, down_proj, down_proj_bias):
        import jax, jax.numpy as jnp
        import numpy as np
        ALPHA = 1.702
        LIMIT = 7.0
        TOP_K = 4
        B, S, H = (1, 128, 256)
        E, D = (16, 256)
        batch, seq, hdim = hidden_states.shape
        x = hidden_states.reshape(-1, hdim)
        T = x.shape[0]
        logits = x @ router_weight.T + router_bias
        top_val, top_idx = jax.lax.top_k(logits, TOP_K)
        top_val = jax.nn.softmax(top_val, axis=-1)
        router_scores = jnp.zeros_like(logits).at[jnp.arange(T)[:, None], top_idx].set(top_val)
        gate_up = jnp.einsum('th,ehd->etd', x, gate_up_proj) + gate_up_proj_bias[:, None, :]
        gate = gate_up[..., ::2]
        up = gate_up[..., 1::2]
        gate = jnp.minimum(gate, LIMIT)
        up = jnp.clip(up, -LIMIT, LIMIT)
        glu = gate * jax.nn.sigmoid(gate * ALPHA)
        out = jnp.einsum('etd,edh->eth', (up + 1.0) * glu, down_proj) + down_proj_bias[:, None, :]
        out = out * router_scores.T[:, :, None]
        out = out.sum(axis=0)
        return out.reshape(batch, seq, hdim)
    x = x + _L0_xattn_ref(_layernorm(x, axis=-1), ctx_2048, ctx_2048, L0_xattn_Wh, L0_xattn_wg_w, L0_xattn_wo_w, L0_xattn_gn_gamma, L0_xattn_gn_beta)
    x = x + _L0_ffn_ref(_layernorm(x, axis=-1), L0_ffn_Wr, L0_ffn_br, L0_ffn_Wg, L0_ffn_Wu, L0_ffn_Wd)
    x = x + _L1_xattn_ref(_layernorm(x, axis=-1), ctx_2048, L1_xattn_context_lens, L1_xattn_Wq, L1_xattn_bq, L1_xattn_gq, L1_xattn_Wk, L1_xattn_bk, L1_xattn_gk, L1_xattn_Wv, L1_xattn_bv, L1_xattn_Wk_img, L1_xattn_bk_img, L1_xattn_gk_img, L1_xattn_Wv_img, L1_xattn_bv_img, L1_xattn_Wo, L1_xattn_bo)
    x = x + _L1_ffn_ref(_layernorm(x, axis=-1), L1_ffn_router_weight, L1_ffn_router_bias, L1_ffn_gate_up_proj, L1_ffn_gate_up_proj_bias, L1_ffn_down_proj, L1_ffn_down_proj_bias)
    return x

_drawn_inputs = setup_inputs


def setup_inputs(seed=0):
    import zlib

    import numpy as np

    out = dict(_drawn_inputs(seed))
    spreads = {'L0_xattn_gn_gamma': (1.0, 0.2),
     'L0_xattn_gn_beta': (0.0, 0.1),
     'L0_ffn_br': (0.0, 0.8),
     'L1_xattn_bq': (0.0, 2.0),
     'L1_xattn_gq': (1.0, 0.6),
     'L1_xattn_bk': (0.0, 0.1),
     'L1_xattn_gk': (1.0, 0.2),
     'L1_xattn_bv': (0.0, 0.1),
     'L1_xattn_bk_img': (0.0, 2.0),
     'L1_xattn_gk_img': (1.0, 0.6),
     'L1_xattn_bv_img': (0.0, 1.918),
     'L1_xattn_bo': (0.0, 0.532)}
    factors = {'L0_ffn_Wr': 7.086,
     'L0_ffn_Wg': 5.848,
     'L0_ffn_Wu': 5.804,
     'L0_ffn_Wd': 5.773,
     'L1_xattn_Wq': 30.792,
     'L1_xattn_Wk_img': 29.424,
     'L1_ffn_router_bias': 64.0,
     'L1_ffn_gate_up_proj_bias': 64.0,
     'L1_ffn_down_proj_bias': 37.356,
     'L1_xattn_Wv_img': 6.185,
     'L1_xattn_Wo': 3.054,
     'L1_ffn_router_weight': 5.779,
     'L1_ffn_gate_up_proj': 8.0,
     'L1_ffn_down_proj': 8.0}
    for name, (base, spread) in spreads.items():
        noise = np.random.default_rng([zlib.crc32(name.encode()), seed]).standard_normal(out[name].shape)
        drawn = base * np.exp(spread * noise) if base else spread * noise
        out[name] = jnp.asarray(drawn.astype(out[name].dtype))
    for name, factor in factors.items():
        out[name] = (out[name] * factor).astype(out[name].dtype)
    return out
```

```python
from contextlib import ExitStack

import concourse.bass as bass
from concourse import mybir
from concourse.alu_op_type import AluOpType as ALU

F32 = mybir.dt.float32
BF16 = mybir.dt.bfloat16
I32 = mybir.dt.int32
U32 = mybir.dt.uint32
ACT = mybir.ActivationFunctionType
X_AXIS = mybir.AxisListType.X

P = 128
B, S, D = 16, 128, 256
T = B * S // P
DC = D // P
TOKENS = B * S
CH = 4
NCH = T // CH
RH, RHD = 2, 128
E0, F0, K0 = 4, 1024, 1
E1, F1, K1 = 16, 256, 4
NB0 = T * K0 + E0 - 1
NB1 = T * K1 + E1
H, HD = 16, 16
LN_EPS, GN_EPS, RMS_EPS = 1e-5, 1e-3, 1e-6

CONST_PARTS = [
    ("ident", P), ("before", P), ("ones", P), ("iota", P), ("decay", RH * P),
    ("expert", E1 * T), ("carry", E1 * T), ("full", E1 * T),
    ("dest0", K0 * T), ("dest1", K1 * T), ("trash0", NB0), ("trash1", NB1),
    ("even_heads", 1), ("odd_heads", 1), ("neg_half", 2 * T), ("lift", P),
]
CONST_AT = {}
CONST_COLS = 0
for _name, _n in CONST_PARTS:
    CONST_AT[_name] = (CONST_COLS, CONST_COLS + _n)
    CONST_COLS += _n


def rounds(eng, start, end):
    yield start
    if end - start > 1:
        with eng.Fori(start + 1, end) as i:
            yield i


class Steps:

    def __init__(self, eng, sem):
        self.eng, self.sem, self.n = eng, sem, 0

    def did(self, ins):
        ins.then_inc(self.sem, 1)
        self.n = self.n + 1
        return self.n

    def wait(self, n=None):
        self.eng.wait_ge(self.sem, self.n if n is None else n)


class Memory:

    def __init__(self, nc, ctx):
        self.nc, self.ctx, self.passing = nc, ctx, []
        self.x = self.sb("x", [P, T, D])
        self.weights = self.sb("weights", [P, 24576])
        self.rows = self.sb("rows", [P, 12544])
        self.stage = self.sb("stage", [P, 5632])
        self.const = self.sb("const", [P, CONST_COLS])
        self.proj = self.sb("proj", [P, 2048])
        self.bias = self.sb("bias", [P, 1536])
        self.router0 = self.sb("router0", [P, DC, E0])
        self.router1 = self.sb("router1", [P, DC, E1])
        self.rbias0 = self.sb("rbias0", [P, E0])
        self.rbias1 = self.sb("rbias1", [P, E1])
        self.stats = self.sb("stats", [P, 2, T, 6])
        self.tmp = self.sb("tmp", [P, 4, 2 * T])
        self.mean = self.sb("mean", [P, T])
        self.rstd = self.sb("rstd", [P, 2 * T])
        self.pick_w = self.sb("pick_w", [P, K1, T])
        self.psum = ctx.enter_context(nc.psum_tensor("psum", [P, 8, 512], F32))
        self.ps = [self.psum[:, i] for i in range(8)]
        self.block_expert = self.sb("block_expert", [1, NB1], I32)
        self.source = self.sb("source", [P, NB1], I32)
        self.dest = self.sb("dest", [P, NB1], I32)

    def sb(self, name, shape, dt=F32):
        return self.ctx.enter_context(self.nc.sbuf_tensor(name, shape, dt))

    def c(self, name):
        a, b = CONST_AT[name]
        return self.const[:, a:b]

    def lasting(self, name):
        return self.nc.alloc_semaphore(name=name)

    def sem(self, name):
        handle = self.nc.alloc_semaphore(name=name)
        self.passing.append(handle)
        return handle

    def recycle(self):
        self.nc.clear_and_free_semaphores(self.passing)
        self.passing = []
        self.nc.all_engine_barrier()


def finish_stats(m, dve, steps, stats, mean, var_eps, eps, n):
    me, de, mo, do = stats[:, :, 1], stats[:, :, 2], stats[:, :, 4], stats[:, :, 5]
    a, b, c, d = (m.tmp[:, i, 0:n] for i in range(4))
    steps.did(dve.tensor_tensor(a, de, do, ALU.add))
    if mean is None:
        steps.did(dve.tensor_tensor(b, me, me, ALU.mult))
        steps.did(dve.tensor_tensor(c, mo, mo, ALU.mult))
        steps.wait()
        steps.did(dve.tensor_scalar(d, a, 1.0 / D, eps, ALU.mult, ALU.add))
        steps.did(dve.tensor_tensor(b, b, c, ALU.add))
        steps.wait()
        return dve.scalar_tensor_tensor(var_eps, b, 0.5, d, ALU.mult, ALU.add)
    steps.did(dve.tensor_tensor(b, me, mo, ALU.subtract))
    steps.did(dve.tensor_tensor(c, me, mo, ALU.add))
    steps.wait()
    steps.did(dve.tensor_tensor(b, b, b, ALU.mult))
    steps.did(dve.tensor_scalar(d, a, 1.0 / D, eps, ALU.mult, ALU.add))
    steps.did(dve.tensor_scalar(mean, c, 0.5, None, ALU.mult))
    steps.wait()
    return dve.scalar_tensor_tensor(var_eps, b, 0.25, d, ALU.mult, ALU.add)


def context_phase(m, a):
    nc = m.nc
    ctx_in = [m.sem(f"ctx_in{i}") for i in range(2)]
    x_in, head_w_in, w_in, late_in = m.sem("x_in"), m.sem("head_w_in"), m.sem("a_w_in"), m.sem("late_in")
    m.x_in, m.a_w_in, m.late_in = x_in, w_in, late_in
    turned, ct_ready, ct_used = m.sem("ctx_turned"), m.sem("ct_ready"), m.sem("ct_used")
    kt_made, v_made = m.sem("kt_made"), m.sem("v_made")
    kt_kept, v_kept = m.sem("kt_kept"), m.sem("v_kept")
    ctx_used = m.sem("ctx_used")
    var_ready, rstd_ready = m.sem("ln0_var_ready"), m.sem("ln0_rstd_ready")
    m.rstd_ready = rstd_ready

    ctx_tiles = m.stage[:, 0:2 * CH * D].rearrange("p (u k d) -> p u k d", u=2, k=CH)
    ct = m.stage[:, 2048:4096].rearrange("p (u c n) -> p u c n", u=2, c=DC)
    kt = m.rows[:, 0:4096].rearrange("p (h n) -> p h n", h=RH)
    v = m.rows[:, 4096:8192].rearrange("p (t n) -> p t n", t=T)
    head_w = m.proj[:, 0:RH * P].rearrange("p (h e) -> p h e", h=RH)
    ident = m.c("ident")
    turn, ktp, vp = m.ps[0:2], m.ps[2:4], m.ps[4:6]
    ctx_rows = a["ctx_2048"].rearrange("(t p) d -> p t d", p=P)
    x_rows = a["x"].rearrange("(t p) d -> p t d", p=P)

    with nc.Block() as block:

        @block.sync
        def _(sp):
            sp.dma_start(m.const[:], a["const"]).then_inc(head_w_in, 16)
            sp.dma_start(head_w, a["L0_xattn_Wh"].rearrange("h d e -> d h e")).then_inc(head_w_in, 16)
            for q in range(NCH):
                if q >= 2:
                    sp.wait_ge(ctx_used, q - 1)
                sp.dma_start(ctx_tiles[:, q % 2], ctx_rows[:, q * CH:(q + 1) * CH]).then_inc(ctx_in[q % 2], 16)
                if q == 1:
                    sp.dma_start(m.x[:, 0:T // 2], x_rows[:, 0:T // 2]).then_inc(x_in, 16)
                    sp.dma_start(m.x[:, T // 2:T], x_rows[:, T // 2:T]).then_inc(x_in, 16)
            wg_w = m.proj[:, 256:768].rearrange("p (c n) -> p c n", c=DC)
            wo_w = m.proj[:, 768:1280].rearrange("p (c n) -> p c n", c=DC)
            sp.dma_start(wg_w, a["L0_xattn_wg_w"].rearrange("(c p) n -> p c n", c=DC)).then_inc(w_in, 16)
            sp.dma_start(wo_w, a["L0_xattn_wo_w"].rearrange("(c p) n -> p c n", c=DC)).then_inc(w_in, 16)
            sp.dma_start(m.bias[:, 0:D], a["L0_xattn_gn_gamma"].partition_broadcast(P)).then_inc(w_in, 16)
            sp.dma_start(m.bias[:, D:2 * D], a["L0_xattn_gn_beta"].partition_broadcast(P)).then_inc(w_in, 16)
            sp.dma_start(m.router0[:], a["L0_ffn_Wr"].rearrange("(c p) e -> p c e", c=DC)).then_inc(late_in, 16)
            sp.dma_start(m.router1[:], a["router1"].rearrange("(c p) e -> p c e", c=DC)).then_inc(late_in, 16)
            sp.dma_start(m.rbias0[:], a["L0_ffn_br"].partition_broadcast(P)).then_inc(late_in, 16)
            sp.dma_start(m.rbias1[:], a["L1_ffn_router_bias"].partition_broadcast(P)).then_inc(late_in, 16)

        @block.tensor
        def _(pe):
            def transposes(q):
                pe.wait_ge(ctx_in[q % 2], 16 * (q // 2 + 1))
                if q >= 1:
                    pe.wait_ge(ct_ready, 2 * q)
                for c in range(DC):
                    for k in range(CH):
                        mm = pe.transpose(turn[c][:, k * P:(k + 1) * P], ctx_tiles[:, q % 2, k, c * P:(c + 1) * P], ident)
                    if c == DC - 1:
                        mm.then_inc(turned, 1)
                        pe.wait_ge(turned, q + 1)
                        pe.sem_inc(ctx_used, 1)

            def products(q):
                pe.wait_ge(ct_ready, 2 * (q + 1))
                if q >= 1:
                    pe.wait_ge(kt_kept, 2 * q)
                for h in range(RH):
                    mm = pe.matmul(ktp[h][:, :], head_w[:, h], ct[:, q % 2, h], start=True, stop=True)
                mm.then_inc(kt_made, 1)
                if q >= 1:
                    pe.wait_ge(v_kept, 2 * q)
                for k in range(CH):
                    for h in range(RH):
                        at = (k % 2) * D + h * P
                        mm = pe.matmul(vp[k // 2][:, at:at + P], ct[:, q % 2, h, k * P:(k + 1) * P], head_w[:, h],
                                       start=True, stop=True)
                mm.then_inc(v_made, 1)

            pe.wait_ge(head_w_in, 32)
            transposes(0)
            for q in range(NCH):
                if q + 1 < NCH:
                    transposes(q + 1)
                products(q)

        @block.scalar
        def _(act):
            for e in range(E0):
                act.dma_start(m.wg0(e), a["L0_ffn_Wg"][e].rearrange("(c p) f -> p c f", c=DC)).then_inc(m.w0_in, 16)
                act.dma_start(m.wu0(e), a["L0_ffn_Wu"][e].rearrange("(c p) f -> p c f", c=DC)).then_inc(m.w0_in, 16)
                act.dma_start(m.wd0(e), a["L0_ffn_Wd"][e].rearrange("(c p) n -> p c n", p=P)).then_inc(m.w0_in, 16)

            def keep_turned(q):
                act.wait_ge(turned, q + 1)
                if q >= 2:
                    act.wait_ge(v_made, q - 1)
                act.copy(ct[:, q % 2, 0], turn[0][:, :]).then_inc(ct_ready, 1)

            def keep_products(q):
                act.wait_ge(kt_made, q + 1)
                act.copy(kt[:, 0, q * 512:(q + 1) * 512], ktp[0][:, :]).then_inc(kt_kept, 1)
                act.wait_ge(v_made, q + 1)
                act.copy(v[:, q * CH:q * CH + 2], vp[0][:, :].rearrange("p (k n) -> p k n", k=2)).then_inc(v_kept, 1)

            keep_turned(0)
            for q in range(NCH):
                if q + 1 < NCH:
                    keep_turned(q + 1)
                keep_products(q)

        @block.vector
        def _(dve):
            steps = m.dve_steps(dve)

            def keep_turned(q):
                dve.wait_ge(turned, q + 1)
                if q >= 2:
                    dve.wait_ge(v_made, q - 1)
                dve.tensor_copy(ct[:, q % 2, 1], turn[1][:, :]).then_inc(ct_ready, 1)

            def keep_products(q):
                dve.wait_ge(kt_made, q + 1)
                dve.tensor_copy(kt[:, 1, q * 512:(q + 1) * 512], ktp[1][:, :]).then_inc(kt_kept, 1)
                dve.wait_ge(v_made, q + 1)
                dve.tensor_copy(v[:, q * CH + 2:q * CH + 4], vp[1][:, :].rearrange("p (k n) -> p k n", k=2)).then_inc(v_kept, 1)

            keep_turned(0)
            for q in range(NCH):
                if q + 1 < NCH:
                    keep_turned(q + 1)
                keep_products(q)
            dve.wait_ge(x_in, 32)
            for t in range(T):
                ins = dve.bn_stats(m.stats[:, 0, t], m.x[:, t])
            steps.did(ins)
            steps.wait()
            finish_stats(m, dve, steps, m.stats[:, 0], m.mean[:], m.tmp[:, 3, 0:T], LN_EPS, T).then_inc(var_ready, 1)

        @block.gpsimd
        def _(pool):
            pool.wait_ge(var_ready, 1)
            pool.wait_ge(head_w_in, 32)
            pool.tensor_tensor(m.rstd[:, 0:T], m.tmp[:, 3, 0:T], m.c("neg_half")[:, 0:T], ALU.pow).then_inc(rstd_ready, 1)


def retention_scores_phase(m, a):
    nc = m.nc
    xn_ready, turned = m.sem("xn_ready"), m.sem("xn_turned")
    xt_ready, qt_made, qt_ready = m.sem("xt_ready"), m.sem("qt_made"), m.sem("qt_ready")
    gate_made, gate_kept, scored = m.sem("gate_made"), m.sem("gate_kept"), m.sem("scored")
    masked, a_turned = m.sem("masked"), m.sem("a_turned")

    xn = m.stage[:, 0:2048].rearrange("p (u k d) -> p u k d", u=2, k=CH)
    xt = m.stage[:, 2048:4096].rearrange("p (u c n) -> p u c n", u=2, c=DC)
    qt = m.stage[:, 4096:5120].rearrange("p (h n) -> p h n", h=RH)
    kt = m.rows[:, 0:4096].rearrange("p (h n) -> p h n", h=RH)
    gate = m.rows[:, 8192:12288].rearrange("p (t n) -> p t n", t=T)
    m.at = m.bias[:, 512:768].rearrange("p (h s) -> p h s", h=RH)
    am = m.bias[:, 768:1024].rearrange("p (h s) -> p h s", h=RH)
    ab = m.bias[:, 1024:1280].rearrange("p (h s) -> p h s", h=RH)
    head_w = m.proj[:, 0:RH * P].rearrange("p (h e) -> p h e", h=RH)
    wg_w = m.proj[:, 256:768].rearrange("p (c n) -> p c n", c=DC)
    ident = m.c("ident")
    decay = m.c("decay").rearrange("p (h n) -> p h n", h=RH)
    turn, qp, gp, sp_ = m.ps[0:2], m.ps[2:4], m.ps[4:6], m.ps[6:8]

    with nc.Block() as block:

        @block.tensor
        def _(pe):
            def transposes(q):
                pe.wait_ge(xn_ready, q + 1)
                if q >= 1:
                    pe.wait_ge(xt_ready, 2 * q)
                for c in range(DC):
                    for k in range(CH):
                        mm = pe.transpose(turn[c][:, k * P:(k + 1) * P], xn[:, q % 2, k, c * P:(c + 1) * P], ident)
                mm.then_inc(turned, 1)

            def products(q):
                pe.wait_ge(xt_ready, 2 * (q + 1))
                if q >= 1:
                    pe.wait_ge(qt_ready, 2 * q)
                for h in range(RH):
                    mm = pe.matmul(qp[h][:, :], head_w[:, h], xt[:, q % 2, h], start=True, stop=True)
                mm.then_inc(qt_made, 1)
                if q >= 1:
                    pe.wait_ge(gate_kept, 2 * q)
                for k in range(CH):
                    for c in range(DC):
                        at = (k % 2) * D
                        mm = pe.matmul(gp[k // 2][:, at:at + D], xt[:, q % 2, c, k * P:(k + 1) * P], wg_w[:, c],
                                       start=(c == 0), stop=(c == DC - 1))
                mm.then_inc(gate_made, 1)
                pe.wait_ge(qt_ready, 2 * (q + 1))
                for h in range(RH):
                    for k in range(CH):
                        b = q * CH + k
                        mm = pe.matmul(sp_[h][:, 0:P], qt[:, h, k * P:(k + 1) * P], kt[:, h, b * P:(b + 1) * P],
                                       start=(b == 0), stop=(b == T - 1))
                mm.then_inc(scored, 1)

            pe.wait_ge(m.a_w_in, 64)
            transposes(0)
            for q in range(NCH):
                if q + 1 < NCH:
                    transposes(q + 1)
                products(q)
            pe.wait_ge(masked, 1)
            for h in range(RH):
                mm = pe.transpose(turn[0][:, h * P:(h + 1) * P], am[:, h], ident)
            mm.then_inc(a_turned, 1)

        @block.scalar
        def _(act):
            def keep_turned(q):
                act.wait_ge(turned, q + 1)
                if q >= 2:
                    act.wait_ge(gate_made, q - 1)
                act.copy(xt[:, q % 2, 0], turn[0][:, :]).then_inc(xt_ready, 1)

            keep_turned(0)
            for q in range(NCH):
                if q + 1 < NCH:
                    keep_turned(q + 1)
                act.wait_ge(qt_made, q + 1)
                if q >= 1:
                    act.wait_ge(scored, q)
                act.copy(qt[:, 0], qp[0][:, :]).then_inc(qt_ready, 1)
                act.wait_ge(gate_made, q + 1)
                for g in range(2):
                    at = q * CH + 2 * g
                    act.activation(gate[:, at:at + 2], gp[g][:, :].rearrange("p (k n) -> p k n", k=2),
                                   ACT.Relu).then_inc(gate_kept, 1)

        @block.vector
        def _(dve):
            steps = m.dve_steps(dve)

            def normalise(q):
                if q >= 2:
                    dve.wait_ge(turned, q - 1)
                for k in range(CH):
                    t = q * CH + k
                    ins = dve.tensor_scalar(xn[:, q % 2, k], m.x[:, t], m.mean[:, t:t + 1], m.rstd[:, t:t + 1],
                                            ALU.subtract, ALU.mult)
                ins.then_inc(xn_ready, 1)

            def keep_turned(q):
                dve.wait_ge(turned, q + 1)
                if q >= 2:
                    dve.wait_ge(gate_made, q - 1)
                dve.tensor_copy(xt[:, q % 2, 1], turn[1][:, :]).then_inc(xt_ready, 1)

            dve.wait_ge(m.rstd_ready, 1)
            normalise(0)
            normalise(1)
            keep_turned(0)
            for q in range(NCH):
                if q + 1 < NCH:
                    keep_turned(q + 1)
                if q + 2 < NCH:
                    normalise(q + 2)
                dve.wait_ge(qt_made, q + 1)
                if q >= 1:
                    dve.wait_ge(scored, q)
                dve.tensor_copy(qt[:, 1], qp[1][:, :]).then_inc(qt_ready, 1)
            dve.wait_ge(scored, NCH)
            for h in range(RH):
                ins = dve.tensor_tensor(am[:, h], sp_[h][:, 0:P], decay[:, h], ALU.mult)
            steps.did(ins)
            steps.wait()
            steps.did(dve.scalar_tensor_tensor(ab[:, :, :], am[:, :, :], -1.0, am[:, :, :], ALU.mult, ALU.max))
            steps.wait()
            dve.tensor_scalar(am[:, :, :], ab[:, :, :], 1.0, None, ALU.max).then_inc(masked, 1)
            dve.wait_ge(a_turned, 1)
            steps.did(dve.tensor_copy(m.at, turn[0][:, 0:RH * P].rearrange("p (h s) -> p h s", h=RH)))
            m.at_step = steps.n


def retention_output_phase(m, a):
    nc = m.nc
    made, kept = m.sem("o_made"), [m.sem(f"o_kept{u}") for u in range(2)]
    var_ready, rstd_ready = m.sem("gn_var_ready"), m.sem("gn_rstd_ready")
    m.gn_rstd_ready = rstd_ready
    v = m.rows[:, 4096:8192].rearrange("p (t h e) -> p t h e", t=T, h=RH)
    o = m.rows[:, 0:4096].rearrange("p (t n) -> p t n", t=T)
    op = m.ps[0:2]

    with nc.Block() as block:

        @block.tensor
        def _(pe):
            pe.wait_ge(m.dve_chain, m.at_step)
            for j in rounds(pe, 0, T // 4):
                for u in range(2):
                    pe.wait_ge(kept[u], j)
                    for h in range(RH):
                        out = op[u][:, :].rearrange("p (k h e) -> p k h e", k=2, h=RH)[:, :, h]
                        mm = pe.matmul(out, m.at[:, h], v[:, bass.ds(j * 4 + 2 * u, 2), h], start=True, stop=True)
                    mm.then_inc(made, 1)

        @block.scalar
        def _(act):
            for j in rounds(act, 0, T // 4):
                for u in range(2):
                    act.wait_ge(made, j * 2 + (u + 1))
                    act.copy(o[:, bass.ds(j * 4 + 2 * u, 2)], op[u][:, :].rearrange("p (k n) -> p k n", k=2)).then_inc(kept[u], 1)

        @block.vector
        def _(dve):
            steps = m.dve_steps(dve)
            base = steps.n
            for j in rounds(dve, 0, T // 4):
                steps.n = base + j * 4
                for u in range(2):
                    dve.wait_ge(kept[u], j + 1)
                    for k in range(2):
                        t = j * 4 + (2 * u + k)
                        steps.did(dve.bn_stats(m.stats[:, 0, bass.ds(t, 1)].rearrange("p a n -> p (a n)"),
                                               o[:, bass.ds(t, 1)].rearrange("p a n -> p (a n)")))
            steps.n = base + T
            steps.wait()
            finish_stats(m, dve, steps, m.stats[:, 0], m.mean[:], m.tmp[:, 3, 0:T], GN_EPS, T).then_inc(var_ready, 1)

        @block.gpsimd
        def _(pool):
            pool.wait_ge(var_ready, 1)
            pool.tensor_tensor(m.rstd[:, 0:T], m.tmp[:, 3, 0:T], m.c("neg_half")[:, 0:T], ALU.pow).then_inc(rstd_ready, 1)


def tile(ap, t):
    return ap[:, bass.ds(t, 1)].rearrange("p a n -> p (a n)")


def col(ap, t):
    return ap[:, bass.ds(t, 1)]


def retention_close_phase(m, a):
    nc = m.nc
    y_norm, y_gated = [[m.sem(f"{n}{u}") for u in range(2)] for n in ("y_norm", "y_gated")]
    y_turned, yt_ready, y_out, x_added = [[m.sem(f"{n}{u}") for u in range(2)] for n in
                                          ("y_turned", "yt_ready", "y_out", "x_added0_")]
    var_ready, rstd_ready = m.sem("ln1_var_ready"), m.sem("ln1_rstd_ready")
    m.ln1_rstd_ready = rstd_ready
    o = m.rows[:, 0:4096].rearrange("p (t n) -> p t n", t=T)
    gate = m.rows[:, 8192:12288].rearrange("p (t n) -> p t n", t=T)
    wo_w = m.proj[:, 768:1280].rearrange("p (c n) -> p c n", c=DC)
    gamma, beta = m.bias[:, 0:D], m.bias[:, D:2 * D]
    y = m.stage[:, 0:512].rearrange("p (u n) -> p u n", u=2)
    z = m.stage[:, 512:1024].rearrange("p (u n) -> p u n", u=2)
    yt = m.stage[:, 1024:1536].rearrange("p (u c n) -> p u c n", u=2, c=DC)
    ident = m.c("ident")
    turn, out = m.ps[0:2], m.ps[2:4]

    with nc.Block() as block:

        @block.vector
        def _(dve):
            steps = m.dve_steps(dve)
            dve.wait_ge(m.gn_rstd_ready, 1)

            def gated(j, u):
                t = j * 2 + u
                dve.wait_ge(y_turned[u], j)
                steps.did(dve.tensor_scalar(y[:, u], tile(o, t), col(m.mean, t), col(m.rstd, t), ALU.subtract, ALU.mult))
                steps.wait()
                steps.did(dve.tensor_tensor(z[:, u], y[:, u], gamma, ALU.mult))
                steps.wait()
                steps.did(dve.tensor_tensor(y[:, u], z[:, u], beta, ALU.add))
                steps.wait()
                dve.tensor_tensor(z[:, u], y[:, u], tile(gate, t), ALU.mult).then_inc(y_gated[u], 1)

            def add(j, u):
                t = j * 2 + u
                dve.wait_ge(y_out[u], j + 1)
                dve.tensor_tensor(tile(m.x, t), tile(m.x, t), out[u][:, 0:D], ALU.add).then_inc(x_added[u], 1)

            def stats(j, u):
                t = j * 2 + u
                dve.wait_ge(x_added[u], j + 1)
                steps.did(dve.bn_stats(tile(m.stats[:, 0], t), tile(m.x, t)))

            base = steps.n
            gated(0, 0)
            gated(0, 1)
            for j in rounds(dve, 0, T // 2 - 1):
                steps.n = base + 6 + j * 8
                for u in range(2):
                    add(j, u)
                    gated(j + 1, u)
                    stats(j, u)
            steps.n = base + 6 + (T // 2 - 1) * 8
            for u in range(2):
                add(T // 2 - 1, u)
                stats(T // 2 - 1, u)
            steps.wait()
            finish_stats(m, dve, steps, m.stats[:, 0], m.mean[:], m.tmp[:, 3, 0:T], LN_EPS, T).then_inc(var_ready, 1)

        @block.tensor
        def _(pe):
            for j in rounds(pe, 0, T // 2):
                for u in range(2):
                    pe.wait_ge(y_gated[u], j + 1)
                    pe.wait_ge(yt_ready[u], j)
                    for c in range(DC):
                        mm = pe.transpose(turn[u][:, c * P:(c + 1) * P], z[:, u, c * P:(c + 1) * P], ident)
                    mm.then_inc(y_turned[u], 1)
                for u in range(2):
                    pe.wait_ge(yt_ready[u], j + 1)
                    pe.wait_ge(x_added[u], j)
                    for c in range(DC):
                        mm = pe.matmul(out[u][:, 0:D], yt[:, u, c], wo_w[:, c], start=(c == 0), stop=(c == DC - 1))
                    mm.then_inc(y_out[u], 1)

        @block.scalar
        def _(act):
            for j in rounds(act, 0, T // 2):
                for u in range(2):
                    act.wait_ge(y_turned[u], j + 1)
                    act.wait_ge(y_out[u], j)
                    act.copy(yt[:, u], turn[u][:, 0:D].rearrange("p (c n) -> p c n", c=DC)).then_inc(yt_ready[u], 1)

        @block.gpsimd
        def _(pool):
            pool.wait_ge(var_ready, 1)
            pool.tensor_tensor(m.rstd[:, 0:T], m.tmp[:, 3, 0:T], m.c("neg_half")[:, 0:T], ALU.pow).then_inc(rstd_ready, 1)


class Layer:

    def __init__(self, n):
        self.n, self.e, self.k, self.nb = n, (E0, E1)[n], (K0, K1)[n], (NB0, NB1)[n]
        self.cols = max(self.e, 8)


def logits_phase(m, a, n):
    nc, L = m.nc, Layer(n)
    sem = lambda name: [m.sem(f"{name}{n}_{u}") for u in range(4)]
    xn_ready, xn_turned, xn_stored = sem("rx_ready"), sem("rx_turned"), sem("rx_stored")
    xt_ready, logit_made, logit_kept = sem("rxt_ready"), sem("logit_made"), sem("logit_kept")
    xn = m.stage[:, 0:1024].rearrange("p (u n) -> p u n", u=4)
    xt = m.stage[:, 1024:2048].rearrange("p (u c n) -> p u c n", u=4, c=DC)
    m.logits = m.rows[:, 0:T * L.cols].rearrange("p (t e) -> p t e", t=T)
    router = (m.router0, m.router1)[n]
    rbias = (m.rbias0, m.rbias1)[n]
    ident = m.c("ident")
    turn, lg = m.ps[0:4], m.ps[4:8]
    xn_rows = a[f"xn{n}"].rearrange("(t p) d -> p t d", p=P)
    turns = T // 4

    with nc.Block() as block:

        @block.vector
        def _(dve):
            steps = m.dve_steps(dve)
            dve.wait_ge(m.ln3_rstd_ready if n else m.ln1_rstd_ready, 1)
            if L.cols > L.e:
                steps.did(dve.memset(m.logits[:, :, L.e:], -3e38))

            def normalise(j, u):
                t = j * 4 + u
                dve.wait_ge(xn_turned[u], j)
                dve.wait_ge(xn_stored[u], j * 16)
                dve.tensor_scalar(xn[:, u], tile(m.x, t), col(m.mean, t), col(m.rstd, t),
                                  ALU.subtract, ALU.mult).then_inc(xn_ready[u], 1)

            def keep(j, u):
                dve.wait_ge(logit_made[u], j + 1)
                dve.tensor_tensor(tile(m.logits, j * 4 + u)[:, 0:L.e], lg[u][:, 0:L.e], rbias[:], ALU.add).then_inc(logit_kept[u], 1)

            for u in range(4):
                normalise(0, u)
            for j in rounds(dve, 0, turns - 1):
                for u in range(4):
                    keep(j, u)
                    normalise(j + 1, u)
            for u in range(4):
                keep(turns - 1, u)

        @block.tensor
        def _(pe):
            if n == 0:
                pe.wait_ge(m.late_in, 64)

            for j in rounds(pe, 0, turns):
                for u in range(4):
                    pe.wait_ge(xn_ready[u], j + 1)
                    pe.wait_ge(xt_ready[u], j)
                    for c in range(DC):
                        mm = pe.transpose(turn[u][:, c * P:(c + 1) * P], xn[:, u, c * P:(c + 1) * P], ident)
                    mm.then_inc(xn_turned[u], 1)
                for u in range(4):
                    pe.wait_ge(xt_ready[u], j + 1)
                    pe.wait_ge(logit_kept[u], j)
                    for c in range(DC):
                        mm = pe.matmul(lg[u][:, 0:L.e], xt[:, u, c], router[:, c], start=(c == 0), stop=(c == DC - 1))
                    mm.then_inc(logit_made[u], 1)

        @block.scalar
        def _(act):
            for j in rounds(act, 0, turns):
                for u in range(4):
                    act.wait_ge(xn_turned[u], j + 1)
                    act.wait_ge(logit_made[u], j)
                    act.copy(xt[:, u], turn[u][:, 0:D].rearrange("p (c n) -> p c n", c=DC)).then_inc(xt_ready[u], 1)

        @block.sync
        def _(sp):
            for j in rounds(sp, 0, turns):
                for u in range(4):
                    sp.wait_ge(xn_ready[u], j + 1)
                    sp.dma_start(xn_rows[:, bass.ds(j * 4 + u, 1)].rearrange("p a n -> p (a n)"), xn[:, u]).then_inc(xn_stored[u], 16)
            for u in range(4):
                sp.wait_ge(xn_stored[u], 16 * turns)


def routing_phase(m, a, n):
    nc, L = m.nc, Layer(n)
    E, K, NB = L.e, L.k, L.nb
    shifted, exped = m.sem(f"shifted{n}"), m.sem(f"exped{n}")
    hot_ready, counted = m.sem(f"hot_ready{n}"), m.sem(f"counted{n}")
    entry_ready, entry_used = [[m.sem(f"{s}{n}_{u}") for u in range(4)] for s in ("entry_ready", "entry_used")]
    table_made = m.sem(f"table_made{n}")

    cursor = [T * L.cols]

    def take(size, dt=F32):
        at = cursor[0]
        cursor[0] += size
        return m.rows[:, at:at + size].bitcast(dt) if dt != F32 else m.rows[:, at:at + size]

    top = take(8 * T).rearrange("p (t k) -> p t k", t=T)
    top_at = take(8 * T, U32).rearrange("p (t k) -> p t k", t=T)
    top_atf = take(8 * T).rearrange("p (t k) -> p t k", t=T)
    wide = E if K == 1 else K
    ex = take(wide * T).rearrange("p (t k) -> p t k", t=T)
    exs = take(T)
    hot = [take(E * T).rearrange("p (e t) -> p e t", e=E) for _ in range(K)]
    hots = hot[0] if K == 1 else take(E * T).rearrange("p (e t) -> p e t", e=E)
    hots2 = take(E * T).rearrange("p (e t) -> p e t", e=E)
    count = take(E * T).rearrange("p (e t) -> p e t", e=E)
    upto = take(E * T).rearrange("p (e t) -> p e t", e=E)
    place = take(E * T).rearrange("p (e t) -> p e t", e=E)
    work = [take(E * T).rearrange("p (e t) -> p e t", e=E) for _ in range(K)]
    blocks, blocks_to, first = take(E), take(E), take(E)
    pos = take(K * T)
    posi, blki = take(K * T, I32), take(K * T, I32)
    blk, row = take(K * T), take(K * T)
    owner = take(NB * E).rearrange("p (b e) -> p b e", b=NB)
    ownf, ownc = take(NB), take(NB)
    tb, gap, tb2 = take(NB), take(NB), take(NB)
    srci = take(NB, I32)
    assert cursor[0] <= 12544
    row_hot = m.stage[:, 0:4 * P].rearrange("p (u s) -> p u s", u=4)
    value = m.stage[:, 512:512 + 4 * NB].rearrange("p (u b) -> p u b", u=4)
    psum_rank, psum_count = m.ps[0][:, 0:E * T], m.ps[1][:, 0:E * T]
    table = m.ps[2][:, 0:NB]
    dest_token = m.c(f"dest{n}")
    entries = K * T // 4

    with nc.Block() as block:

        @block.vector
        def _(dve):
            steps = m.dve_steps(dve)
            did, wait = steps.did, steps.wait
            for t in range(T):
                ins = dve.max(top[:, t], m.logits[:, t])
            did(ins)
            wait()
            for t in range(T):
                ins = dve.max_index(top_at[:, t], top[:, t], m.logits[:, t])
            did(ins)
            best = top[:, :, 0:1].to_broadcast([P, T, wide])
            dve.tensor_tensor(ex, m.logits[:, :, 0:E] if K == 1 else top[:, :, 0:K], best, ALU.subtract).then_inc(shifted, 1)
            wait()
            did(dve.tensor_copy(top_atf, top_at))
            wait()
            experts = m.c("expert")[:, 0:E * T].rearrange("p (e t) -> p e t", e=E)
            for k in range(K):
                ins = dve.tensor_tensor(hot[k], experts, top_atf[:, :, k].unsqueeze(1).to_broadcast([P, E, T]), ALU.is_equal)
            did(ins)
            wait()
            if K == 1:
                dve.sem_inc(hot_ready, 1)
            else:
                did(dve.tensor_tensor(hots2, hot[0], hot[1], ALU.add))
                did(dve.tensor_tensor(place, hot[2], hot[3], ALU.add))
                wait()
                dve.tensor_tensor(hots, hots2, place, ALU.add).then_inc(hot_ready, 1)
            dve.wait_ge(exped, 1)
            did(dve.tensor_reduce(exs, ex, X_AXIS, ALU.add))
            wait()
            if K == 1:
                did(dve.reciprocal(m.pick_w[:, 0], exs))
            else:
                did(dve.reciprocal(exs, exs))
                wait()
                did(dve.tensor_tensor(m.pick_w[:, 0:K].rearrange("p k t -> p t k"), ex,
                                      exs.unsqueeze(2).to_broadcast([P, T, K]), ALU.mult))
            dve.wait_ge(counted, 1)
            did(dve.tensor_copy(count, psum_count.rearrange("p (e t) -> p e t", e=E)))
            wait()
            flat = lambda ap: ap.rearrange("p e t -> p (e t)")
            did(dve.tensor_tensor_scan(flat(upto), m.c("carry")[:, 0:E * T], flat(count), 0.0, ALU.mult, ALU.add))
            wait()
            did(dve.tensor_tensor(work[0], m.c("full")[:, 0:E * T].rearrange("p (e t) -> p e t", e=E),
                                  upto[:, :, T - 1:T].to_broadcast([P, E, T]), ALU.is_lt))
            did(dve.tensor_tensor(place, upto, count, ALU.subtract))
            wait()
            did(dve.tensor_reduce(blocks, work[0], X_AXIS, ALU.add))
            did(dve.tensor_tensor(hots2, place, psum_rank.rearrange("p (e t) -> p e t", e=E), ALU.add))
            wait()
            did(dve.tensor_tensor_scan(blocks_to, m.c("ones")[:, 0:E], blocks, 0.0, ALU.mult, ALU.add))
            wait()
            did(dve.tensor_tensor(first, blocks_to, blocks, ALU.subtract))
            did(dve.tensor_tensor(owner[0:1], blocks_to[0:1].unsqueeze(1).to_broadcast([1, NB, E]),
                                  m.c("iota")[0:1, 0:NB].unsqueeze(2).to_broadcast([1, NB, E]), ALU.is_le))
            wait()
            did(dve.scalar_tensor_tensor(place, first.unsqueeze(2).to_broadcast([P, E, T]), float(P), hots2, ALU.mult, ALU.add))
            did(dve.tensor_reduce(ownf[0:1], owner[0:1], X_AXIS, ALU.add))
            wait()
            for k in range(K):
                ins = dve.tensor_tensor(work[k], hot[k], place, ALU.mult)
            did(ins)
            did(dve.tensor_scalar(m.block_expert[:, 0:NB], ownf[0:1], float(E - 1), None, ALU.min))
            wait()
            for k in range(K):
                ins = dve.tensor_reduce(pos[:, k * T:(k + 1) * T], work[k].rearrange("p e t -> p t e"), X_AXIS, ALU.add)
            did(ins)
            wait()
            did(dve.tensor_copy(posi, pos))
            wait()
            did(dve.tensor_single_scalar(blki, posi, 7, ALU.arith_shift_right))
            wait()
            did(dve.tensor_copy(blk, blki))
            wait()
            did(dve.scalar_tensor_tensor(row, blk, -float(P), pos, ALU.mult, ALU.add))
            wait()

            def entry(j, u):
                i = j * 4 + u
                dve.wait_ge(entry_used[u], j)
                did(dve.tensor_scalar(row_hot[:, u], m.c("iota"), col(row, i), None, ALU.is_equal))
                dve.tensor_scalar(value[:, u], m.c("iota")[:, 0:NB], col(blk, i), col(dest_token, i),
                                  ALU.is_equal, ALU.mult).then_inc(entry_ready[u], 1)

            base = steps.n
            for j in rounds(dve, 0, entries):
                steps.n = base + j * 4
                for u in range(4):
                    entry(j, u)
            steps.n = base + entries * 4
            dve.wait_ge(table_made, 1)
            did(dve.tensor_scalar(gap, table, 0.5, None, ALU.is_lt))
            did(dve.tensor_scalar(tb, table, -1.0, None, ALU.add))
            wait()
            did(dve.tensor_tensor(gap, gap, m.c(f"trash{n}"), ALU.mult))
            did(dve.tensor_scalar(srci, tb, 0.0, None, ALU.max))
            wait()
            did(dve.tensor_tensor(m.dest[:, 0:NB], gap, tb, ALU.add))
            did(dve.tensor_single_scalar(m.source[:, 0:NB], srci, K.bit_length() - 1, ALU.arith_shift_right))

        @block.scalar
        def _(act):
            act.wait_ge(shifted, 1)
            act.activation(ex, ex, ACT.Exp).then_inc(exped, 1)

        @block.tensor
        def _(pe):
            pe.wait_ge(hot_ready, 1)
            flat = hots.rearrange("p e t -> p (e t)")
            pe.matmul(psum_rank, m.c("before"), flat, start=True, stop=True)
            pe.matmul(psum_count, m.c("ones"), flat, start=True, stop=True).then_inc(counted, 1)

            def entry(j, u, start=False, stop=False):
                pe.wait_ge(entry_ready[u], j + 1)
                return pe.matmul(table, row_hot[:, u], value[:, u], start=start, stop=stop)

            for u in range(4):
                entry(0, u, start=(u == 0)).then_inc(entry_used[u], 1)
            for j in rounds(pe, 1, entries - 1):
                for u in range(4):
                    entry(j, u).then_inc(entry_used[u], 1)
            for u in range(4):
                mm = entry(entries - 1, u, stop=(u == 3))
            mm.then_inc(table_made, 1)


def gather_and_scatter(m, pool, a, n, rows_in, rows_in_sem, rows_taken, out, out_ready, stored, nb, bufs, lag):
    for b in range(nb + lag):
        if b < nb:
            i = b % bufs
            if b >= bufs:
                pool.wait_ge(rows_taken[i], b // bufs)
            pool.indirect_dma_start(rows_in[:, i], None, a[f"xn{n}"],
                                    bass.IndirectOffsetOnAxis(ap=m.source[:, b:b + 1], axis=0)).then_inc(rows_in_sem[i], 16)
        d = b - lag
        if d >= 0:
            i = d % bufs
            pool.wait_ge(out_ready[i], d // bufs + 1)
            pool.indirect_dma_start(a[f"y{n}"], bass.IndirectOffsetOnAxis(ap=m.dest[:, d:d + 1], axis=0),
                                    out[:, i], None).then_inc(stored[i], 16)
    for i in range(bufs):
        pool.wait_ge(stored[i], 16 * ((nb - i + bufs - 1) // bufs))


def experts0_phase(m, a):
    nc = m.nc
    NB, FH = NB0, F0 // 2
    FC = FH // P
    sem = m.sem
    BUFS = 1
    rows_in = [sem(f"e0_in{i}") for i in range(BUFS)]
    stored = [sem(f"e0_stored{i}") for i in range(BUFS)]
    turned, xt_ready = sem("e0_turned"), sem("e0_xt_ready")
    gu_made, sig_ready, h_ready = [[sem(f"{s}{u}") for u in range(2)] for s in ("e0_gu", "e0_sig", "e0_h")]
    h_turned, ht_ready, down_made = [[sem(f"{s}{u}") for u in range(2)] for s in ("e0_ht", "e0_htr", "e0_down")]
    y_ready = sem("e0_y_ready")
    m.c_w_in = m.lasting("c_w_in")
    part = m.rows[:, 0:4096]
    xg = m.stage[:, 0:256].rearrange("p (u n) -> p u n", u=1)
    xt = m.stage[:, 256:512].rearrange("p (c n) -> p c n", c=DC)
    yo = m.stage[:, 512:768].rearrange("p (u n) -> p u n", u=1)
    sig = part[:, 0:1024].rearrange("p (u n) -> p u n", u=2)
    prod = part[:, 1024:2048].rearrange("p (u n) -> p u n", u=2)
    hid = part[:, 2048:3072].rearrange("p (u n) -> p u n", u=2)
    ht = part[:, 3072:4096].rearrange("p (u c n) -> p u c n", u=2, c=FC)
    g_ps = [m.ps[0], m.ps[2]]
    u_ps = [m.ps[1], m.ps[3]]
    x_turn, h_turn, y_ps = m.ps[4], m.ps[5], m.ps[6]
    ident = m.c("ident")
    wg = m.weights[:, 0:8192].rearrange("p (e c f) -> p e c f", e=E0, c=DC)
    wu = m.weights[:, 8192:16384].rearrange("p (e c f) -> p e c f", e=E0, c=DC)
    wd = m.weights[:, 16384:24576].rearrange("p (e c n) -> p e c n", e=E0, c=F0 // P)

    with nc.Block() as block:

        @block.gpsimd
        def _(pool):
            gather_and_scatter(m, pool, a, 0, xg, rows_in, [turned], yo, [y_ready], stored, NB, BUFS, 2)

        @block.sync
        def _(sp):
            for i, w in enumerate(("Wq", "Wk_img", "Wv_img", "Wo")):
                sp.dma_start(m.proj[:, i * 512:(i + 1) * 512].rearrange("p (c n) -> p c n", c=DC),
                             a[f"L1_xattn_{w}"].rearrange("(c p) n -> p c n", c=DC)).then_inc(m.c_w_in, 16)
            for i, w in enumerate(("bq", "bk_img", "gq", "gk_img", "bv_img", "bo")):
                sp.dma_start(m.bias[:, i * D:(i + 1) * D], a[f"L1_xattn_{w}"].partition_broadcast(P)).then_inc(m.c_w_in, 16)

        @block.tensor
        def _(pe):
            def turn_rows(b):
                pe.wait_ge(rows_in[0], 16 * (b + 1))
                pe.wait_ge(xt_ready, b)
                for c in range(DC):
                    mm = pe.transpose(x_turn[:, c * P:(c + 1) * P], xg[:, 0, c * P:(c + 1) * P], ident)
                mm.then_inc(turned, 1)

            def gate_up(b, e, u):
                if u == 0:
                    pe.wait_ge(xt_ready, b + 1)
                pe.wait_ge(h_ready[u], b)
                for w, ps in ((wg, g_ps[u]), (wu, u_ps[u])):
                    for c in range(DC):
                        rhs = w[:, bass.ds(e, 1), c, u * FH:(u + 1) * FH].rearrange("p a f -> p (a f)")
                        mm = pe.matmul(ps[:, :], xt[:, c], rhs, start=(c == 0), stop=(c == DC - 1))
                mm.then_inc(gu_made[u], 1)

            def turn_hidden(b, u):
                pe.wait_ge(h_ready[u], b + 1)
                if u == 0:
                    pe.wait_ge(ht_ready[1], b)
                else:
                    pe.wait_ge(ht_ready[0], b + 1)
                for c in range(FC):
                    mm = pe.transpose(h_turn[:, c * P:(c + 1) * P], hid[:, u, c * P:(c + 1) * P], ident)
                mm.then_inc(h_turned[u], 1)

            def down(b, e, u):
                pe.wait_ge(ht_ready[u], b + 1)
                if u == 0:
                    pe.wait_ge(y_ready, b)
                for c in range(FC):
                    rhs = wd[:, bass.ds(e, 1), u * FC + c].rearrange("p a n -> p (a n)")
                    mm = pe.matmul(y_ps[:, 0:D], ht[:, u, c], rhs, start=(u == 0 and c == 0), stop=(u == 1 and c == FC - 1))
                mm.then_inc(down_made[u], 1)

            def expert(b):
                return pe.value_load(m.block_expert[0:1, bass.ds(b, 1)], min_val=0, max_val=E0 - 1)

            def step(b, last=False):
                e, e_before = expert(b), expert(b - 1)
                turn_hidden(b - 1, 0)
                gate_up(b, e, 0)
                down(b - 1, e_before, 0)
                turn_hidden(b - 1, 1)
                gate_up(b, e, 1)
                if not last:
                    turn_rows(b + 1)
                down(b - 1, e_before, 1)

            pe.wait_ge(m.w0_in, 16 * 3 * E0)
            turn_rows(0)
            e = expert(0)
            gate_up(0, e, 0)
            gate_up(0, e, 1)
            turn_rows(1)
            for b in rounds(pe, 1, NB - 1):
                step(b)
            step(NB - 1, last=True)
            e = expert(NB - 1)
            for u in range(2):
                turn_hidden(NB - 1, u)
                down(NB - 1, e, u)

        @block.scalar
        def _(act):
            def sigmoid(b, u):
                act.wait_ge(gu_made[u], b + 1)
                act.activation(sig[:, u], g_ps[u][:, :], ACT.Sigmoid).then_inc(sig_ready[u], 1)

            def keep_hidden(b, u):
                act.wait_ge(h_turned[u], b + 1)
                act.copy(ht[:, u], h_turn[:, :].rearrange("p (c n) -> p c n", c=FC)).then_inc(ht_ready[u], 1)

            def keep_rows(b):
                act.wait_ge(turned, b + 1)
                act.wait_ge(gu_made[1], b)
                act.copy(xt[:, :], x_turn[:, 0:D].rearrange("p (c n) -> p c n", c=DC)).then_inc(xt_ready, 1)

            def keep_out(b):
                act.wait_ge(down_made[1], b + 1)
                act.wait_ge(stored[0], b * 16)
                act.copy(yo[:, 0], y_ps[:, 0:D]).then_inc(y_ready, 1)

            keep_rows(0)
            sigmoid(0, 0)
            sigmoid(0, 1)
            keep_rows(1)

            def step(b, last=False):
                keep_hidden(b - 1, 0)
                sigmoid(b, 0)
                keep_hidden(b - 1, 1)
                sigmoid(b, 1)
                if not last:
                    keep_rows(b + 1)
                keep_out(b - 1)

            for b in rounds(act, 1, NB - 1):
                step(b)
            step(NB - 1, last=True)
            keep_hidden(NB - 1, 0)
            keep_hidden(NB - 1, 1)
            keep_out(NB - 1)

        @block.vector
        def _(dve):
            steps = m.dve_steps(dve)
            base = steps.n
            for b in rounds(dve, 0, NB):
                steps.n = base + b * 2
                for u in range(2):
                    dve.wait_ge(sig_ready[u], b + 1)
                    steps.did(dve.tensor_tensor(prod[:, u], g_ps[u][:, :], sig[:, u], ALU.mult))
                    steps.wait()
                    dve.wait_ge(h_turned[u], b)
                    dve.tensor_tensor(hid[:, u], u_ps[u][:, :], prod[:, u], ALU.mult).then_inc(h_ready[u], 1)
            steps.n = base + NB * 2


def combine_phase(m, a, n):
    nc, L = m.nc, Layer(n)
    K = L.k
    sem = lambda name: [m.sem(f"{name}{n}_{u}") for u in range(4)]
    y_in, x_ready, out_done = sem("y_in"), sem("xc_ready"), sem("out_done")
    var_ready = m.sem(f"c_var_ready{n}")
    if n == 0:
        m.ln2_rstd_ready = m.lasting("ln2_rstd_ready")
        m.w1_in = m.lasting("w1_in")
    y = m.stage[:, 0:4 * K * D].rearrange("p (u k d) -> p u k d", u=4, k=K)
    y_rows = a[f"y{n}"][0:TOKENS * K].rearrange("(t p k) d -> p t (k d)", p=P, k=K)
    out_rows = a["out"].rearrange("(t p) d -> p t d", p=P)
    turns = T // 4

    with nc.Block() as block:

        @block.sync
        def _(sp):
            for j in rounds(sp, 0, turns):
                for u in range(4):
                    sp.wait_ge(x_ready[u], j)
                    sp.dma_start(y[:, u].rearrange("p k d -> p (k d)"),
                                 y_rows[:, bass.ds(j * 4 + u, 1)].rearrange("p a n -> p (a n)")).then_inc(y_in[u], 16)

        @block.vector
        def _(dve):
            steps = m.dve_steps(dve)
            base = steps.n
            per = 4 * (K - 1) + (4 if n == 0 else 0)
            for j in rounds(dve, 0, turns):
                steps.n = base + j * per
                for k in range(K):
                    for u in range(4):
                        t = j * 4 + u
                        if k == 0:
                            dve.wait_ge(y_in[u], j * 16 + 16)
                        else:
                            steps.wait(base + j * per + ((k - 1) * 4 + u + 1))
                        ins = dve.scalar_tensor_tensor(tile(m.x, t), y[:, u, k], col(m.pick_w[:, k], t), tile(m.x, t),
                                                       ALU.mult, ALU.add)
                        if k == K - 1:
                            ins.then_inc(x_ready[u], 1)
                        else:
                            steps.did(ins)
                if n == 0:
                    for u in range(4):
                        t = j * 4 + u
                        dve.wait_ge(x_ready[u], j + 1)
                        steps.did(dve.bn_stats(tile(m.stats[:, 0], t), tile(m.x, t)))
            steps.n = base + turns * per
            if n == 0:
                steps.wait()
                finish_stats(m, dve, steps, m.stats[:, 0], m.mean[:], m.tmp[:, 3, 0:T], LN_EPS, T).then_inc(var_ready, 1)

        if n == 0:
            @block.gpsimd
            def _(pool):
                pool.wait_ge(var_ready, 1)
                pool.tensor_tensor(m.rstd[:, 0:T], m.tmp[:, 3, 0:T], m.c("neg_half")[:, 0:T], ALU.pow).then_inc(m.ln2_rstd_ready, 1)

        @block.scalar
        def _(act):
            if n == 0:
                for e in range(E1):
                    act.dma_start(m.weights[:, e * 1024:(e + 1) * 1024].rearrange("p (c f) -> p c f", c=DC),
                                  a["L1_ffn_gate_up_proj"][e].rearrange("(c p) f -> p c f", c=DC)).then_inc(m.w1_in, 16)
                    act.dma_start(m.weights[:, 16384 + e * 512:16384 + (e + 1) * 512].rearrange("p (c n) -> p c n", c=DC),
                                  a["L1_ffn_down_proj"][e].rearrange("(c p) n -> p c n", c=DC)).then_inc(m.w1_in, 16)
            else:
                for j in rounds(act, 0, turns):
                    for u in range(4):
                        act.wait_ge(x_ready[u], j + 1)
                        act.dma_start(out_rows[:, bass.ds(j * 4 + u, 1)].rearrange("p a n -> p (a n)"),
                                      tile(m.x, j * 4 + u)).then_inc(out_done[u], 16)
                for u in range(4):
                    act.wait_ge(out_done[u], 16 * turns)


VW = HD + 1


def projections_phase(m, a):
    nc, sem = m.nc, m.sem
    ctx_in = [sem(f"c_ctx_in{u}") for u in range(2)]
    xn_ready, turned, xt_ready = sem("c_xn_ready"), sem("c_turned"), sem("c_xt_ready")
    qk_made, v_made, qk_kept, v_kept = sem("qk_made"), sem("v_made1"), sem("qk_kept"), sem("v_kept1")
    biased = sem("bo_added")
    var_ready = sem("rms_var_ready")
    m.rms_ready = sem("rms_ready")
    xn = m.stage[:, 0:512].rearrange("p (u n) -> p u n", u=2)
    cx = m.stage[:, 512:1024].rearrange("p (u n) -> p u n", u=2)
    xct = m.stage[:, 1024:2048].rearrange("p (u w c n) -> p u w c n", u=2, w=2, c=DC)
    qk = m.rows[:, 0:8192].rearrange("p (t n) -> p t n", t=T)
    v = m.rows[:, 8192:12544].rearrange("p (t h d) -> p t h d", t=T, h=H)
    wq, wk, wv = (m.proj[:, i * 512:(i + 1) * 512].rearrange("p (c n) -> p c n", c=DC) for i in range(3))
    bqk, bv, bo = m.bias[:, 0:2 * D], m.bias[:, 4 * D:5 * D], m.bias[:, 5 * D:6 * D]
    turn, qkp, vp = m.ps[0:2], m.ps[2:4], m.ps[4:6]
    ident = m.c("ident")
    ctx_rows = a["ctx_2048"].rearrange("(t p) d -> p t d", p=P)

    with nc.Block() as block:

        @block.sync
        def _(sp):
            for j in rounds(sp, 0, T // 2):
                for u in range(2):
                    t = j * 2 + u
                    sp.wait_ge(xt_ready, t)
                    sp.dma_start(cx[:, u], ctx_rows[:, bass.ds(t, 1)].rearrange("p a n -> p (a n)")).then_inc(ctx_in[u], 16)

        @block.vector
        def _(dve):
            steps = m.dve_steps(dve)
            dve.wait_ge(m.ln2_rstd_ready, 1)
            steps.did(dve.memset(v[:, :, :, HD:VW], 1.0))
            dve.wait_ge(m.c_w_in, 160)

            def normalise(t, u):
                dve.tensor_scalar(xn[:, u], tile(m.x, t), col(m.mean, t), col(m.rstd, t),
                                  ALU.subtract, ALU.mult).then_inc(xn_ready, 1)

            def keep(t, u):
                dve.wait_ge(qk_made, t + 1)
                dve.tensor_tensor(tile(qk, t), qkp[u][:, :], bqk, ALU.add).then_inc(qk_kept, 1)
                dve.wait_ge(v_made, t + 1)
                dve.tensor_tensor(v[:, bass.ds(t, 1), :, 0:HD].rearrange("p a h d -> p (a h) d"),
                                  vp[u][:, 0:D].rearrange("p (h d) -> p h d", h=H),
                                  bv.rearrange("p (h d) -> p h d", h=H), ALU.add).then_inc(v_kept, 1)
                dve.wait_ge(qk_kept, t + 1)
                for w in range(2):
                    steps.did(dve.bn_stats(tile(m.stats[:, w], t), tile(qk, t)[:, w * D:(w + 1) * D]))

            normalise(0, 0)
            normalise(1, 1)
            base = steps.n
            for j in rounds(dve, 0, T // 2 - 1):
                steps.n = base + j * 4
                for u in range(2):
                    t = j * 2 + u
                    keep(t, u)
                    dve.wait_ge(turned, t + 1)
                    normalise(t + 2, u)
            steps.n = base + (T // 2 - 1) * 4
            for u in range(2):
                keep(T - 2 + u, u)
            steps.wait()
            finish_stats(m, dve, steps, m.stats[:, :].rearrange("p w t s -> p (w t) s"), None, m.tmp[:, 3],
                         RMS_EPS, 2 * T).then_inc(var_ready, 1)

        @block.tensor
        def _(pe):
            def turn_tile(j, t, u):
                pe.wait_ge(xn_ready, t + 1)
                pe.wait_ge(ctx_in[u], j * 16 + 16)
                pe.wait_ge(xt_ready, t)
                for w, src in enumerate((xn, cx)):
                    for c in range(DC):
                        at = (w * DC + c) * P
                        mm = pe.transpose(turn[u][:, at:at + P], src[:, u, c * P:(c + 1) * P], ident)
                mm.then_inc(turned, 1)

            def products(t, u):
                pe.wait_ge(xt_ready, t + 1)
                pe.wait_ge(v_kept, t)
                for w, (src, wt) in enumerate(((0, wq), (1, wk))):
                    for c in range(DC):
                        mm = pe.matmul(qkp[u][:, w * D:(w + 1) * D], xct[:, u, src, c], wt[:, c], start=(c == 0), stop=(c == DC - 1))
                mm.then_inc(qk_made, 1)
                for c in range(DC):
                    mm = pe.matmul(vp[u][:, 0:D], xct[:, u, 1, c], wv[:, c], start=(c == 0), stop=(c == DC - 1))
                mm.then_inc(v_made, 1)

            turn_tile(0, 0, 0)
            for j in rounds(pe, 0, T // 2 - 1):
                turn_tile(j, j * 2 + 1, 1)
                products(j * 2, 0)
                turn_tile(j + 1, j * 2 + 2, 0)
                products(j * 2 + 1, 1)
            turn_tile(T // 2 - 1, T - 1, 1)
            products(T - 2, 0)
            products(T - 1, 1)

        @block.scalar
        def _(act):
            def keep_turned(t, u):
                act.wait_ge(turned, t + 1)
                act.copy(xct[:, u], turn[u][:, :].rearrange("p (w c n) -> p w c n", w=2, c=DC)).then_inc(xt_ready, 1)

            keep_turned(0, 0)
            keep_turned(1, 1)
            for j in rounds(act, 1, T // 2):
                for u in range(2):
                    t = j * 2 + u
                    act.wait_ge(v_made, t - 1)
                    keep_turned(t, u)

        @block.gpsimd
        def _(pool):
            for t in rounds(pool, 0, T):
                pool.wait_ge(xn_ready, t + 1)
                pool.tensor_tensor(tile(m.x, t), tile(m.x, t), bo, ALU.add).then_inc(biased, 1)
            pool.wait_ge(biased, T)
            pool.wait_ge(var_ready, 1)
            pool.tensor_tensor(m.rstd[:], m.tmp[:, 3], m.c("neg_half"), ALU.pow).then_inc(m.rms_ready, 1)


def attention_phase(m, a):
    nc, sem = m.nc, m.sem
    qn_ready, qk_turned, k_ready = sem("qn_ready"), sem("qk_turned"), sem("k_ready")
    scored, shifted, exped = sem("s_scored"), sem("s_shifted"), sem("s_exped")
    p_turned, pt_even, pt_odd, pv_made = sem("p_turned"), sem("pt_even"), sem("pt_odd"), sem("pv_made")
    o_ready, o_turned, ot_ready, wo_made, x_added = sem("o_ready"), sem("o_turned"), sem("ot_ready"), sem("wo_made"), sem("x_added")
    var_ready = sem("ln3_var_ready")
    m.ln3_rstd_ready = sem("ln3_rstd_ready")
    G = 4
    HG = H // G

    def head(g, i):
        return (i // 2) * (H // 2) + 2 * g + i % 2

    s = m.stage
    qn = s[:, 0:1024].rearrange("p (u n) -> p u n", u=2)
    qt = s[:, 1024:1280].rearrange("p (c n) -> p c n", c=DC)
    kt = s[:, 1280:1792].rearrange("p (c z n) -> p c z n", c=DC, z=2)
    prob = s[:, 1792:3840]
    pt = s[:, 3840:4864].rearrange("p (v n) -> p v n", v=2)
    o = s[:, 4864:5120]
    ot = s[:, 5120:5376].rearrange("p (c n) -> p c n", c=DC)
    top, inv = s[:, 5376:5376 + H], s[:, 5400:5400 + H]
    qk = m.rows[:, 0:8192].rearrange("p (t n) -> p t n", t=T)
    v = m.rows[:, 8192:12544].rearrange("p (t h d) -> p t h d", t=T, h=H)
    wo = m.proj[:, 1536:2048].rearrange("p (c n) -> p c n", c=DC)
    gq, gk = m.bias[:, 2 * D:3 * D], m.bias[:, 3 * D:4 * D]
    scores = m.psum[:, 0:G].rearrange("p g n -> p (g n)").rearrange("p (h n) -> p h n", h=H)
    pt_ps, pv_ps, turn = m.ps[4:6], m.ps[6], m.ps[7]
    pv = pv_ps[:, 0:H * VW].rearrange("p (h d) -> p h d", h=H)
    ident = m.c("ident")

    with nc.Block() as block:

        @block.vector
        def _(dve):
            steps = m.dve_steps(dve)
            dve.wait_ge(m.rms_ready, 1)

            def norm_qk(t, u):
                if not isinstance(t, int) or t >= 2:
                    dve.wait_ge(qk_turned, t - 1)
                dve.scalar_tensor_tensor(qn[:, u, 0:D], tile(qk, t)[:, 0:D], col(m.rstd[:, 0:T], t), gq, ALU.mult, ALU.mult)
                dve.scalar_tensor_tensor(qn[:, u, D:2 * D], tile(qk, t)[:, D:2 * D], col(m.rstd[:, T:2 * T], t), gk,
                                         ALU.mult, ALU.mult).then_inc(qn_ready, 1)

            def find_top(t):
                dve.wait_ge(scored, t + 1)
                steps.did(dve.tensor_reduce(top, scores, X_AXIS, ALU.max))

            def shift(t, n):
                steps.wait(n)
                dve.wait_ge(p_turned, t * G)
                dve.tensor_tensor(prob.rearrange("p (h n) -> p h n", h=H), scores,
                                  top.unsqueeze(2).to_broadcast([P, H, S]), ALU.subtract).then_inc(shifted, 1)

            def keep_pt(t, g):
                dve.wait_ge(p_turned, t * G + (g + 1))
                if g >= 2 or not isinstance(t, int) or t >= 1:
                    dve.wait_ge(pv_made, t * G + (g - 1))
                dve.tensor_copy(pt[:, g % 2], pt_ps[g % 2][:, :]).then_inc(pt_odd, 1)

            def normed_out(t):
                dve.wait_ge(pv_made, t * G + G)
                steps.did(dve.reciprocal(inv.unsqueeze(2), pv[:, :, HD:VW]))
                steps.wait()
                dve.wait_ge(o_turned, t)
                dve.tensor_tensor(o.rearrange("p (h d) -> p h d", h=H), pv[:, :, 0:HD],
                                  inv.unsqueeze(2).to_broadcast([P, H, HD]), ALU.mult).then_inc(o_ready, 1)

            def add(t):
                dve.wait_ge(wo_made, t + 1)
                dve.tensor_tensor(tile(m.x, t), tile(m.x, t), pt_ps[1][:, 0:D], ALU.add).then_inc(x_added, 1)

            def stats(t):
                dve.wait_ge(x_added, t + 1)
                steps.did(dve.bn_stats(tile(m.stats[:, 0], t), tile(m.x, t)))

            def step(t, u, before, after2, after1=True):
                if after2:
                    norm_qk(t + 2, u)
                if after1:
                    find_top(t + 1)
                top_at = steps.n
                if before:
                    add(t - 1)
                keep_pt(t, 1)
                keep_pt(t, 3)
                if after1:
                    shift(t + 1, top_at)
                normed_out(t)
                if before:
                    stats(t - 1)

            norm_qk(0, 0)
            norm_qk(1, 1)
            find_top(0)
            shift(0, steps.n)
            step(0, 0, False, True)
            step(1, 1, True, True)
            base = steps.n
            for j in rounds(dve, 1, T // 2 - 1):
                for u in range(2):
                    steps.n = base + (j - 1) * 6 + 3 * u
                    step(j * 2 + u, u, True, True)
            steps.n = base + (T // 2 - 2) * 6
            step(T - 2, 0, True, False)
            step(T - 1, 1, True, False, False)
            add(T - 1)
            stats(T - 1)
            steps.wait()
            finish_stats(m, dve, steps, m.stats[:, 0], m.mean[:], m.tmp[:, 3, 0:T], LN_EPS, T).then_inc(var_ready, 1)

        @block.tensor
        def _(pe):
            def turn_qk(t, u):
                pe.wait_ge(qn_ready, t + 1)
                pe.wait_ge(k_ready, t)
                for i in range(4):
                    mm = pe.transpose(turn[:, i * P:(i + 1) * P], qn[:, u, i * P:(i + 1) * P], ident)
                mm.then_inc(qk_turned, 1)

            def score(t):
                pe.wait_ge(k_ready, t + 1)
                pe.wait_ge(shifted, t)
                for c in range(DC):
                    for g in range(G):
                        strip = slice(32 * g, 32 * g + 32)
                        mm = pe.matmul(m.ps[g][:, c * 2 * S:(c + 1) * 2 * S], qt[strip, c],
                                       kt[strip, c].rearrange("p z n -> p (z n)"), start=True, stop=True)
                mm.then_inc(scored, 1)

            def turn_probs(t, g):
                if g == 0:
                    pe.wait_ge(exped, t + 1)
                    pe.wait_ge(ot_ready, t)
                if g == 1:
                    pe.wait_ge(x_added, t)
                if g >= 2:
                    pe.wait_ge((pt_even, pt_odd)[g % 2], t * 2 + 1)
                for i in range(HG):
                    at = g * HG + i
                    mm = pe.transpose(pt_ps[g % 2][:, i * P:(i + 1) * P], prob[:, at * P:(at + 1) * P], ident)
                mm.then_inc(p_turned, 1)

            def values(t, g):
                pe.wait_ge((pt_even, pt_odd)[g % 2], t * 2 + (g // 2 + 1))
                if g == 0:
                    pe.wait_ge(o_ready, t)
                for i in range(HG):
                    h = head(g, i)
                    mm = pe.matmul(pv[:, h], pt[:, g % 2, i * P:(i + 1) * P],
                                   v[:, bass.ds(t, 1), h].rearrange("p a d -> p (a d)"), start=True, stop=True)
                mm.then_inc(pv_made, 1)

            def turn_out(t):
                pe.wait_ge(o_ready, t + 1)
                for c in range(DC):
                    mm = pe.transpose(pt_ps[0][:, c * P:(c + 1) * P], o[:, c * P:(c + 1) * P], ident)
                mm.then_inc(o_turned, 1)

            def project(t):
                pe.wait_ge(ot_ready, t + 1)
                for c in range(DC):
                    mm = pe.matmul(pt_ps[1][:, 0:D], ot[:, c], wo[:, c], start=(c == 0), stop=(c == DC - 1))
                mm.then_inc(wo_made, 1)

            def step(t, u, before, after2, after1=True):
                if after1:
                    score(t + 1)
                if before:
                    turn_out(t - 1)
                if after2:
                    turn_qk(t + 2, u)
                if before:
                    project(t - 1)
                turn_probs(t, 0)
                turn_probs(t, 1)
                values(t, 0)
                turn_probs(t, 2)
                values(t, 1)
                turn_probs(t, 3)
                values(t, 2)
                values(t, 3)

            turn_qk(0, 0)
            score(0)
            turn_qk(1, 1)
            step(0, 0, False, True)
            step(1, 1, True, True)
            for j in rounds(pe, 1, T // 2 - 1):
                for u in range(2):
                    step(j * 2 + u, u, True, True)
            step(T - 2, 0, True, False)
            step(T - 1, 1, True, False, False)
            turn_out(T - 1)
            project(T - 1)

        @block.scalar
        def _(act):
            def keep_qk(t):
                act.wait_ge(qk_turned, t + 1)
                act.wait_ge(scored, t)
                act.copy(qt, turn[:, 0:D].rearrange("p (c n) -> p c n", c=DC))
                ktp = turn[:, D:2 * D].rearrange("p (c n) -> p c n", c=DC)
                act.activation(kt[:, :, 0], ktp, ACT.Copy, scale=m.c("even_heads"))
                act.activation(kt[:, :, 1], ktp, ACT.Copy, scale=m.c("odd_heads")).then_inc(k_ready, 1)

            def exp(t):
                act.wait_ge(shifted, t + 1)
                act.activation(prob, prob, ACT.Exp, scale=float(HD) ** -0.5).then_inc(exped, 1)

            def keep_pt(t, g):
                act.wait_ge(p_turned, t * G + (g + 1))
                if g >= 2 or not isinstance(t, int) or t >= 1:
                    act.wait_ge(pv_made, t * G + (g - 1))
                act.copy(pt[:, g % 2], pt_ps[g % 2][:, :]).then_inc(pt_even, 1)

            def keep_out(t):
                act.wait_ge(o_turned, t + 1)
                act.wait_ge(wo_made, t)
                act.copy(ot, pt_ps[0][:, 0:D].rearrange("p (c n) -> p c n", c=DC)).then_inc(ot_ready, 1)

            def step(t, before, after2, after1=True):
                if before:
                    keep_out(t - 1)
                if after2:
                    keep_qk(t + 2)
                keep_pt(t, 0)
                keep_pt(t, 2)
                if after1:
                    exp(t + 1)

            keep_qk(0)
            keep_qk(1)
            exp(0)
            step(0, False, True)
            step(1, True, True)
            for j in rounds(act, 1, T // 2 - 1):
                for u in range(2):
                    step(j * 2 + u, True, True)
            step(T - 2, True, False)
            step(T - 1, True, False, False)
            keep_out(T - 1)

        @block.gpsimd
        def _(pool):
            pool.wait_ge(var_ready, 1)
            pool.tensor_tensor(m.rstd[:, 0:T], m.tmp[:, 3, 0:T], m.c("neg_half")[:, 0:T], ALU.pow).then_inc(m.ln3_rstd_ready, 1)


def experts1_phase(m, a):
    nc, sem = m.nc, m.sem
    NB, BUFS = NB1, 4
    PAIRS = NB // 2
    LIMIT, ALPHA = 7.0, 1.702
    rows_in = [sem(f"e1_in{i}") for i in range(BUFS)]
    stored = [sem(f"e1_stored{i}") for i in range(BUFS)]
    taken = [sem(f"e1_taken{i}") for i in range(BUFS)]
    out_ready = [sem(f"e1_out{i}") for i in range(BUFS)]
    bias_in, bias_split, bias_rows = sem("e1_bias_in"), sem("e1_bias_split"), sem("e1_bias_rows")
    bias_out = sem("e1_bias_out")
    turned, xt_ready, gu_made = sem("e1_turned"), sem("e1_xt_ready"), sem("e1_gu_made")
    gate_ready, sig_ready, h_ready = sem("e1_gate_ready"), sem("e1_sig_ready"), sem("e1_h_ready")
    h_turned, ht_ready, down_made, y_kept = sem("e1_h_turned"), sem("e1_ht_ready"), sem("e1_down_made"), sem("e1_y_kept")
    ones_ready = sem("e1_ones_ready")

    r, s = m.rows, m.stage
    gub = r[0:3, 0:4096].bitcast(BF16)
    db = r[0:3, 4096:6144].bitcast(BF16)
    xg = r[:, 6144:7168].rearrange("p (i n) -> p i n", i=BUFS)
    yo = r[:, 7168:8192].rearrange("p (i n) -> p i n", i=BUFS)
    gate, up, sig, upg = (r[:, at:at + 1024].rearrange("p (u w n) -> p u w n", u=2, w=2)
                          for at in (8192, 9216, 10240, 11264))
    ones3 = r[0:3, 12288:12352].bitcast(BF16)
    raw, rest = s[:, 3072:3168], s[:, 3168:3264]
    split = s[:, 3264:3408].bitcast(BF16).rearrange("p (i n) -> p i n", i=3)
    hid = s[:, 0:1024].rearrange("p (u w n) -> p u w n", u=2, w=2)
    xt = s[:, 1024:2048].rearrange("p (u w c n) -> p u w c n", u=2, w=2, c=DC)
    ht = s[:, 2048:3072].rearrange("p (u w c n) -> p u w c n", u=2, w=2, c=DC)
    gu = [m.psum[:, 2 * u:2 * u + 2] for u in range(2)]
    x_turn, h_turn, y_ps = m.ps[4], m.ps[5], m.ps[6]
    ident = m.c("ident")
    wgu = m.weights[:, 0:16384].rearrange("p (e c f) -> p e c f", e=E1, c=DC)
    wd = m.weights[:, 16384:24576].rearrange("p (e c n) -> p e c n", e=E1, c=DC)

    with nc.Block() as block:

        @block.sync
        def _(sp):
            sp.dma_start(raw[:, 0:64], a["L1_ffn_gate_up_proj_bias"].rearrange("e f -> (e f)").rearrange("(p n) -> p n", p=P)).then_inc(bias_in, 16)
            sp.dma_start(raw[:, 64:96], a["L1_ffn_down_proj_bias"].rearrange("e f -> (e f)").rearrange("(p n) -> p n", p=P)).then_inc(bias_in, 16)
            gu_parts, d_parts = a["bias_parts"][:, 0:E1 * 2 * F1], a["bias_parts"][:, E1 * 2 * F1:]
            sp.wait_ge(bias_split, 3)
            sp.dma_start(gu_parts.rearrange("i (p n) -> p i n", p=P), split[:, :, 0:64]).then_inc(bias_out, 16)
            sp.dma_start(d_parts.rearrange("i (p n) -> p i n", p=P), split[:, :, 64:96]).then_inc(bias_out, 16)
            sp.wait_ge(bias_out, 32)
            sp.dma_start(gub, gu_parts).then_inc(bias_rows, 16)
            sp.dma_start(db, d_parts).then_inc(bias_rows, 16)

        @block.gpsimd
        def _(pool):
            gather_and_scatter(m, pool, a, 1, xg, rows_in, taken, yo, out_ready, stored, NB, BUFS, 8)

        @block.vector
        def _(dve):
            steps = m.dve_steps(dve)
            dve.memset(ones3, 1.0).then_inc(ones_ready, 1)
            dve.wait_ge(bias_in, 32)
            left = raw
            for i in range(3):
                dve.tensor_copy(split[:, i], left).then_inc(bias_split, 1)
                if i < 2:
                    dve.wait_ge(bias_split, i + 1)
                    steps.did(dve.tensor_tensor(rest, left, split[:, i], ALU.subtract))
                    steps.wait()
                    left = rest
            base = steps.n
            for j in rounds(dve, 0, PAIRS // 2):
                steps.n = base + j * 4
                for u in range(2):
                    p = j * 2 + u
                    dve.wait_ge(gu_made, p + 1)
                    dve.tensor_scalar(gate[:, u], gu[u][:, :, 0:F1], LIMIT, None, ALU.min).then_inc(gate_ready, 1)
                    steps.did(dve.tensor_scalar(up[:, u], gu[u][:, :, F1:2 * F1], LIMIT, -LIMIT, ALU.min, ALU.max))
                    dve.wait_ge(sig_ready, p + 1)
                    steps.wait()
                    steps.did(dve.scalar_tensor_tensor(upg[:, u], up[:, u], 1.0, sig[:, u], ALU.add, ALU.mult))
                    steps.wait()
                    dve.wait_ge(h_turned, p)
                    dve.tensor_tensor(hid[:, u], upg[:, u], gate[:, u], ALU.mult).then_inc(h_ready, 1)

        @block.tensor
        def _(pe):
            def turn_rows(j, p, u):
                pe.wait_ge(xt_ready, p)
                for w in range(2):
                    i = 2 * u + w
                    pe.wait_ge(rows_in[i], j * 16 + 16)
                    for c in range(DC):
                        at = (w * DC + c) * P
                        mm = pe.transpose(x_turn[:, at:at + P], xg[:, i, c * P:(c + 1) * P], ident)
                    mm.then_inc(taken[i], 1)

            def gate_up(p, experts, u):
                pe.wait_ge(xt_ready, p + 1)
                if not isinstance(p, int) or p >= 2:
                    pe.wait_ge(h_ready, p - 1)
                for w, e in enumerate(experts):
                    pe.matmul(gu[u][:, w], ones3, gub[:, bass.ds(e * 2 * F1, 2 * F1)], start=True, stop=False)
                    for c in range(DC):
                        rhs = wgu[:, bass.ds(e, 1), c].rearrange("p a f -> p (a f)")
                        mm = pe.matmul(gu[u][:, w], xt[:, u, w, c], rhs, start=False, stop=(c == DC - 1))
                mm.then_inc(gu_made, 1)

            def turn_hidden(p, u):
                pe.wait_ge(h_ready, p + 1)
                pe.wait_ge(ht_ready, p)
                for w in range(2):
                    for c in range(DC):
                        at = (w * DC + c) * P
                        mm = pe.transpose(h_turn[:, at:at + P], hid[:, u, w, c * P:(c + 1) * P], ident)
                mm.then_inc(h_turned, 1)

            def down(p, experts, u):
                pe.wait_ge(ht_ready, p + 1)
                pe.wait_ge(y_kept, p)
                for w, e in enumerate(experts):
                    out = y_ps[:, w * D:(w + 1) * D]
                    pe.matmul(out, ones3, db[:, bass.ds(e * D, D)], start=True, stop=False)
                    for c in range(DC):
                        rhs = wd[:, bass.ds(e, 1), c].rearrange("p a n -> p (a n)")
                        mm = pe.matmul(out, ht[:, u, w, c], rhs, start=False, stop=(c == DC - 1))
                mm.then_inc(down_made, 1)

            def experts(p):
                return [pe.value_load(m.block_expert[0:1, bass.ds(p * 2 + w, 1)], min_val=0, max_val=E1 - 1) for w in range(2)]

            def step(j, u, last=False):
                p = j * 2 + u
                e, e_before = experts(p), experts(p - 2)
                turn_hidden(p - 2, u)
                gate_up(p, e, u)
                if not last:
                    turn_rows(j + u, p + 1, 1 - u)
                down(p - 2, e_before, u)

            pe.wait_ge(m.w1_in, 16 * 2 * E1)
            pe.wait_ge(ones_ready, 1)
            pe.wait_ge(bias_rows, 32)
            turn_rows(0, 0, 0)
            gate_up(0, experts(0), 0)
            turn_rows(0, 1, 1)
            gate_up(1, experts(1), 1)
            turn_rows(1, 2, 0)
            for j in rounds(pe, 1, PAIRS // 2 - 1):
                step(j, 0)
                step(j, 1)
            step(PAIRS // 2 - 1, 0)
            step(PAIRS // 2 - 1, 1, last=True)
            for u in range(2):
                p = PAIRS - 2 + u
                turn_hidden(p, u)
                down(p, experts(p), u)

        @block.scalar
        def _(act):
            def keep_rows(p, u):
                act.wait_ge(taken[2 * u + 1], p // 2 + 1 if isinstance(p, int) else p)
                act.copy(xt[:, u], x_turn[:, :].rearrange("p (w c n) -> p w c n", w=2, c=DC)).then_inc(xt_ready, 1)

            def sigmoid(p, u):
                act.wait_ge(gate_ready, p + 1)
                act.activation(sig[:, u], gate[:, u], ACT.Sigmoid, scale=ALPHA).then_inc(sig_ready, 1)

            def keep_hidden(p, u):
                act.wait_ge(h_turned, p + 1)
                act.copy(ht[:, u], h_turn[:, :].rearrange("p (w c n) -> p w c n", w=2, c=DC)).then_inc(ht_ready, 1)

            def keep_out(j, p, u):
                act.wait_ge(down_made, p + 1)
                for w in range(2):
                    i = 2 * u + w
                    act.wait_ge(stored[i], j * 16)
                    ins = act.copy(yo[:, i], y_ps[:, w * D:(w + 1) * D])
                    ins.then_inc(out_ready[i], 1)
                    act.wait_ge(out_ready[i], j + 1)
                act.sem_inc(y_kept, 1)

            def step(j, u, last=False):
                p = j * 2 + u
                keep_hidden(p - 2, u)
                sigmoid(p, u)
                if not last:
                    act.wait_ge(taken[2 * (1 - u) + 1], j + u + 1)
                    act.copy(xt[:, 1 - u], x_turn[:, :].rearrange("p (w c n) -> p w c n", w=2, c=DC)).then_inc(xt_ready, 1)
                keep_out(j - 1, p - 2, u)

            keep_rows(0, 0)
            keep_rows(1, 1)
            sigmoid(0, 0)
            act.wait_ge(taken[1], 2)
            act.wait_ge(gu_made, 1)
            act.copy(xt[:, 0], x_turn[:, :].rearrange("p (w c n) -> p w c n", w=2, c=DC)).then_inc(xt_ready, 1)
            sigmoid(1, 1)
            for j in rounds(act, 1, PAIRS // 2 - 1):
                step(j, 0)
                step(j, 1)
            step(PAIRS // 2 - 1, 0)
            step(PAIRS // 2 - 1, 1, last=True)
            for u in range(2):
                keep_hidden(PAIRS - 2 + u, u)
                keep_out(PAIRS // 2 - 1, PAIRS - 2 + u, u)


SCRATCH = [("xn0", TOKENS), ("y0", TOKENS * K0 + P * NB0), ("xn1", TOKENS), ("y1", TOKENS * K1 + P * NB1)]


def first_experts(m, a):
    logits_phase(m, a, 0)
    routing_phase(m, a, 0)
    experts0_phase(m, a)
    combine_phase(m, a, 0)
    m.recycle()


def second_experts(m, a):
    logits_phase(m, a, 1)
    routing_phase(m, a, 1)
    experts1_phase(m, a)
    combine_phase(m, a, 1)


PHASES = [context_phase, retention_scores_phase, retention_output_phase, retention_close_phase,
          first_experts, projections_phase, attention_phase, second_experts]


def build(nc, a, phases=None):
    with ExitStack() as ctx:
        m = Memory(nc, ctx)
        m.w0_in = m.lasting("w0_in")
        m.dve_chain = m.lasting("dve_chain")
        m.all_steps = {}
        m.act_table = None

        def dve_steps(eng):
            if "dve" not in m.all_steps:
                m.all_steps["dve"] = Steps(eng, m.dve_chain)
            m.all_steps["dve"].eng = eng
            return m.all_steps["dve"]

        m.dve_steps = dve_steps
        wg = m.weights[:, 0:8192].rearrange("p (e c f) -> p e c f", e=E0, c=DC)
        wu = m.weights[:, 8192:16384].rearrange("p (e c f) -> p e c f", e=E0, c=DC)
        wd = m.weights[:, 16384:24576].rearrange("p (e c n) -> p e c n", e=E0, c=F0 // P)
        m.wg0, m.wu0, m.wd0 = (lambda e: wg[:, e]), (lambda e: wu[:, e]), (lambda e: wd[:, e])
        for phase in PHASES[:phases]:
            phase(m, a)


def constants():
    import numpy as np
    c = {}
    i = np.arange(P)
    c["ident"] = np.eye(P)
    c["before"] = (i[:, None] < i[None, :])
    c["ones"] = np.ones((P, P))
    c["iota"] = np.tile(i, (P, 1))
    g = (1.0 - 2.0 ** (-5.0 - np.arange(RH, dtype=np.float64)))
    expo = i[None, :] - i[:, None]
    dm = np.where(expo[None] <= 0, g[:, None, None] ** expo[None].astype(np.float64), 0.0)
    dn = dm / np.sqrt(dm.sum(-1))[:, None, :] / np.sqrt(float(RHD))
    c["decay"] = dn.transpose(1, 0, 2).reshape(P, -1)
    et = np.zeros((E1, T))
    c["expert"] = np.tile((et + np.arange(E1)[:, None]).reshape(1, -1), (P, 1))
    c["carry"] = np.tile((et + (np.arange(T) > 0)).reshape(1, -1), (P, 1))
    c["full"] = np.tile((et + P * np.arange(T)).reshape(1, -1), (P, 1))
    token = i[:, None] + P * np.arange(T)[None, :]
    c["dest0"] = token + 1
    c["dest1"] = (token[:, None, :] * K1 + np.arange(K1)[None, :, None] + 1).reshape(P, -1)
    c["trash0"] = TOKENS * K0 + 1 + P * np.arange(NB0)[None, :] + i[:, None]
    c["trash1"] = TOKENS * K1 + 1 + P * np.arange(NB1)[None, :] + i[:, None]
    c["even_heads"] = ((i // HD) % 2 == 0)[:, None]
    c["odd_heads"] = ((i // HD) % 2 == 1)[:, None]
    c["neg_half"] = np.full((P, 2 * T), -0.5)
    c["lift"] = np.zeros((P, P))
    return np.ascontiguousarray(np.concatenate([c[n] for n, _ in CONST_PARTS], axis=1).astype(np.float32))


_SKIP = ("L1_xattn_context_lens", "L1_xattn_Wk", "L1_xattn_bk", "L1_xattn_gk", "L1_xattn_Wv", "L1_xattn_bv",
         "L1_ffn_router_weight")


def layout(inputs):
    import numpy as np
    arrays = {}
    for name, v in inputs.items():
        if name in _SKIP:
            continue
        arrays[name] = np.ascontiguousarray(v)
    arrays["x"] = arrays["x"].reshape(TOKENS, D)
    arrays["ctx_2048"] = arrays["ctx_2048"].reshape(TOKENS, D)
    gu = arrays["L1_ffn_gate_up_proj"].reshape(E1, D, F1, 2)
    arrays["L1_ffn_gate_up_proj"] = np.ascontiguousarray(gu.transpose(0, 1, 3, 2)).reshape(E1, D, 2 * F1)
    gb = arrays["L1_ffn_gate_up_proj_bias"].reshape(E1, F1, 2)
    arrays["L1_ffn_gate_up_proj_bias"] = np.ascontiguousarray(gb.transpose(0, 2, 1)).reshape(E1, 2 * F1)
    arrays["router1"] = np.ascontiguousarray(np.asarray(inputs["L1_ffn_router_weight"]).T)
    arrays["const"] = constants()
    return arrays


def kernel(**inputs):
    import concourse.bacc as bacc
    from concourse.bass_utils import run_bass_kernel_spmd

    nc = bacc.Bacc("TRN2", target_bir_lowering=False, num_devices=1)
    arrays = layout(inputs)
    a = {n: nc.dram_tensor(f"in_{n}", v.shape, mybir.dt.from_np(v.dtype), kind="ExternalInput").ap()
         for n, v in arrays.items()}
    a["out"] = nc.dram_tensor("out", (TOKENS, D), F32, kind="ExternalOutput").ap()
    for name, rows in SCRATCH:
        a[name] = nc.dram_tensor(name, (rows, D), F32, kind="Internal").ap()
    a["bias_parts"] = nc.dram_tensor("bias_parts", (3, E1 * (2 * F1 + D)), BF16, kind="Internal").ap()
    build(nc, a)
    r = run_bass_kernel_spmd(nc, [{f"in_{n}": v for n, v in arrays.items()}], core_ids=[0])
    return r.results[0]["out"].reshape(B, S, D)
```

```python
from contextlib import ExitStack

import concourse.bass as bass
from concourse import mybir
from concourse.alu_op_type import AluOpType as ALU

F32 = mybir.dt.float32
BF16 = mybir.dt.bfloat16
I32 = mybir.dt.int32
U32 = mybir.dt.uint32
ACT = mybir.ActivationFunctionType
X_AXIS = mybir.AxisListType.X

P = 128
B, S, D = 16, 128, 256
T = B * S // P
DC = D // P
TOKENS = B * S
CH = 4
NCH = T // CH
RH, RHD = 2, 128
E0, F0, K0 = 4, 1024, 1
E1, F1, K1 = 16, 256, 4
NB0 = T * K0 + E0 - 1
NB1 = T * K1 + E1
H, HD = 16, 16
LN_EPS, GN_EPS, RMS_EPS = 1e-5, 1e-3, 1e-6

CONST_PARTS = [
    ("ident", P), ("before", P), ("ones", P), ("iota", P), ("decay", RH * P),
    ("expert", E1 * T), ("carry", E1 * T), ("full", E1 * T),
    ("dest0", K0 * T), ("dest1", K1 * T), ("trash0", NB0), ("trash1", NB1),
    ("heads", H // 2), ("neg_half", 2 * T),
]
CONST_AT = {}
CONST_COLS = 0
for _name, _n in CONST_PARTS:
    CONST_AT[_name] = (CONST_COLS, CONST_COLS + _n)
    CONST_COLS += _n


def rounds(eng, start, end):
    yield start
    if end - start > 1:
        with eng.Fori(start + 1, end) as i:
            yield i


class Steps:

    def __init__(self, eng, sem):
        self.eng, self.sem, self.n = eng, sem, 0

    def did(self, ins):
        ins.then_inc(self.sem, 1)
        self.n = self.n + 1
        return self.n

    def wait(self, n=None):
        self.eng.wait_ge(self.sem, self.n if n is None else n)


class Memory:

    def __init__(self, nc, ctx):
        self.nc, self.ctx, self.passing = nc, ctx, []
        self.x = self.sb("x", [P, T, D])
        self.weights = self.sb("weights", [P, 24576])
        self.rows = self.sb("rows", [P, 12416])
        self.stage = self.sb("stage", [P, 5632])
        self.const = self.sb("const", [P, CONST_COLS])
        self.proj = self.sb("proj", [P, 2048])
        self.bias = self.sb("bias", [P, 1536])
        self.router0 = self.sb("router0", [P, DC, E0])
        self.router1 = self.sb("router1", [P, DC, E1])
        self.rbias0 = self.sb("rbias0", [P, E0])
        self.rbias1 = self.sb("rbias1", [P, E1])
        self.stats = self.sb("stats", [P, 2, T, 6])
        self.tmp = self.sb("tmp", [P, 4, 2 * T])
        self.mean = self.sb("mean", [P, T])
        self.rstd = self.sb("rstd", [P, 2 * T])
        self.pick_w = self.sb("pick_w", [P, K1, T])
        self.psum = ctx.enter_context(nc.psum_tensor("psum", [P, 8, 512], F32))
        self.ps = [self.psum[:, i] for i in range(8)]
        self.block_expert = self.sb("block_expert", [1, NB1], I32)
        self.source = self.sb("source", [P, NB1], I32)
        self.dest = self.sb("dest", [P, NB1], I32)

    def sb(self, name, shape, dt=F32):
        return self.ctx.enter_context(self.nc.sbuf_tensor(name, shape, dt))

    def c(self, name):
        a, b = CONST_AT[name]
        return self.const[:, a:b]

    def lasting(self, name):
        return self.nc.alloc_semaphore(name=name)

    def sem(self, name):
        handle = self.nc.alloc_semaphore(name=name)
        self.passing.append(handle)
        return handle

    def recycle(self):
        self.nc.clear_and_free_semaphores(self.passing)
        self.passing = []
        self.nc.all_engine_barrier()


def finish_stats(m, dve, steps, stats, mean, var_eps, eps, n):
    me, de, mo, do = stats[:, :, 1], stats[:, :, 2], stats[:, :, 4], stats[:, :, 5]
    a, b, c, d = (m.tmp[:, i, 0:n] for i in range(4))
    steps.did(dve.tensor_tensor(a, de, do, ALU.add))
    if mean is None:
        steps.did(dve.tensor_tensor(b, me, me, ALU.mult))
        steps.did(dve.tensor_tensor(c, mo, mo, ALU.mult))
        steps.wait()
        steps.did(dve.tensor_scalar(d, a, 1.0 / D, eps, ALU.mult, ALU.add))
        steps.did(dve.tensor_tensor(b, b, c, ALU.add))
        steps.wait()
        return dve.scalar_tensor_tensor(var_eps, b, 0.5, d, ALU.mult, ALU.add)
    steps.did(dve.tensor_tensor(b, me, mo, ALU.subtract))
    steps.did(dve.tensor_tensor(c, me, mo, ALU.add))
    steps.wait()
    steps.did(dve.tensor_tensor(b, b, b, ALU.mult))
    steps.did(dve.tensor_scalar(d, a, 1.0 / D, eps, ALU.mult, ALU.add))
    steps.did(dve.tensor_scalar(mean, c, 0.5, None, ALU.mult))
    steps.wait()
    return dve.scalar_tensor_tensor(var_eps, b, 0.25, d, ALU.mult, ALU.add)


def context_phase(m, a):
    nc = m.nc
    ctx_in = [m.sem(f"ctx_in{i}") for i in range(2)]
    x_in, head_w_in, w_in, late_in = m.sem("x_in"), m.sem("head_w_in"), m.sem("a_w_in"), m.sem("late_in")
    m.x_in, m.a_w_in, m.late_in = x_in, w_in, late_in
    turned, ct_ready, ct_used = m.sem("ctx_turned"), m.sem("ct_ready"), m.sem("ct_used")
    kt_made, v_made = m.sem("kt_made"), m.sem("v_made")
    kt_kept, v_kept = m.sem("kt_kept"), m.sem("v_kept")
    ctx_used = m.sem("ctx_used")
    var_ready, rstd_ready = m.sem("ln0_var_ready"), m.sem("ln0_rstd_ready")
    m.rstd_ready = rstd_ready

    ctx_tiles = m.stage[:, 0:2 * CH * D].rearrange("p (u k d) -> p u k d", u=2, k=CH)
    ct = m.stage[:, 2048:4096].rearrange("p (u c n) -> p u c n", u=2, c=DC)
    kt = m.rows[:, 0:4096].rearrange("p (h n) -> p h n", h=RH)
    v = m.rows[:, 4096:8192].rearrange("p (t n) -> p t n", t=T)
    head_w = m.proj[:, 0:RH * P].rearrange("p (h e) -> p h e", h=RH)
    ident = m.c("ident")
    turn, ktp, vp = m.ps[0:2], m.ps[2:4], m.ps[4:6]
    ctx_rows = a["ctx_2048"].rearrange("(t p) d -> p t d", p=P)
    x_rows = a["x"].rearrange("(t p) d -> p t d", p=P)

    with nc.Block() as block:

        @block.sync
        def _(sp):
            sp.dma_start(m.const[:], a["const"]).then_inc(head_w_in, 16)
            sp.dma_start(head_w, a["L0_xattn_Wh"].rearrange("h d e -> d h e")).then_inc(head_w_in, 16)
            for q in range(NCH):
                if q >= 2:
                    sp.wait_ge(ctx_used, q - 1)
                sp.dma_start(ctx_tiles[:, q % 2], ctx_rows[:, q * CH:(q + 1) * CH]).then_inc(ctx_in[q % 2], 16)
                if q == 1:
                    sp.dma_start(m.x[:, 0:T // 2], x_rows[:, 0:T // 2]).then_inc(x_in, 16)
                    sp.dma_start(m.x[:, T // 2:T], x_rows[:, T // 2:T]).then_inc(x_in, 16)
            wg_w = m.proj[:, 256:768].rearrange("p (c n) -> p c n", c=DC)
            wo_w = m.proj[:, 768:1280].rearrange("p (c n) -> p c n", c=DC)
            sp.dma_start(wg_w, a["L0_xattn_wg_w"].rearrange("(c p) n -> p c n", c=DC)).then_inc(w_in, 16)
            sp.dma_start(wo_w, a["L0_xattn_wo_w"].rearrange("(c p) n -> p c n", c=DC)).then_inc(w_in, 16)
            sp.dma_start(m.bias[:, 0:D], a["L0_xattn_gn_gamma"].partition_broadcast(P)).then_inc(w_in, 16)
            sp.dma_start(m.bias[:, D:2 * D], a["L0_xattn_gn_beta"].partition_broadcast(P)).then_inc(w_in, 16)
            sp.dma_start(m.router0[:], a["L0_ffn_Wr"].rearrange("(c p) e -> p c e", c=DC)).then_inc(late_in, 16)
            sp.dma_start(m.router1[:], a["router1"].rearrange("(c p) e -> p c e", c=DC)).then_inc(late_in, 16)
            sp.dma_start(m.rbias0[:], a["L0_ffn_br"].partition_broadcast(P)).then_inc(late_in, 16)
            sp.dma_start(m.rbias1[:], a["L1_ffn_router_bias"].partition_broadcast(P)).then_inc(late_in, 16)

        @block.tensor
        def _(pe):
            def transposes(q):
                pe.wait_ge(ctx_in[q % 2], 16 * (q // 2 + 1))
                if q >= 1:
                    pe.wait_ge(ct_ready, 2 * q)
                for c in range(DC):
                    for k in range(CH):
                        mm = pe.transpose(turn[c][:, k * P:(k + 1) * P], ctx_tiles[:, q % 2, k, c * P:(c + 1) * P], ident)
                    if c == DC - 1:
                        mm.then_inc(turned, 1)
                        pe.wait_ge(turned, q + 1)
                        pe.sem_inc(ctx_used, 1)

            def products(q):
                pe.wait_ge(ct_ready, 2 * (q + 1))
                if q >= 1:
                    pe.wait_ge(kt_kept, 2 * q)
                for h in range(RH):
                    mm = pe.matmul(ktp[h][:, :], head_w[:, h], ct[:, q % 2, h], start=True, stop=True)
                mm.then_inc(kt_made, 1)
                if q >= 1:
                    pe.wait_ge(v_kept, 2 * q)
                for k in range(CH):
                    for h in range(RH):
                        at = (k % 2) * D + h * P
                        mm = pe.matmul(vp[k // 2][:, at:at + P], ct[:, q % 2, h, k * P:(k + 1) * P], head_w[:, h],
                                       start=True, stop=True)
                mm.then_inc(v_made, 1)

            pe.wait_ge(head_w_in, 32)
            transposes(0)
            for q in range(NCH):
                if q + 1 < NCH:
                    transposes(q + 1)
                products(q)

        @block.scalar
        def _(act):
            def load_experts():
                act.wait_ge(x_in, 32)
                for e in range(E0):
                    act.dma_start(m.wg0(e), a["L0_ffn_Wg"][e].rearrange("(c p) f -> p c f", c=DC)).then_inc(m.w0_in, 16)
                    act.dma_start(m.wu0(e), a["L0_ffn_Wu"][e].rearrange("(c p) f -> p c f", c=DC)).then_inc(m.w0_in, 16)
                    act.dma_start(m.wd0(e), a["L0_ffn_Wd"][e].rearrange("(c p) n -> p c n", p=P)).then_inc(m.w0_in, 16)

            def keep_turned(q):
                act.wait_ge(turned, q + 1)
                if q >= 2:
                    act.wait_ge(v_made, q - 1)
                act.copy(ct[:, q % 2, 0], turn[0][:, :]).then_inc(ct_ready, 1)

            def keep_products(q):
                act.wait_ge(kt_made, q + 1)
                act.copy(kt[:, 0, q * 512:(q + 1) * 512], ktp[0][:, :]).then_inc(kt_kept, 1)
                act.wait_ge(v_made, q + 1)
                act.copy(v[:, q * CH:q * CH + 2], vp[0][:, :].rearrange("p (k n) -> p k n", k=2)).then_inc(v_kept, 1)

            keep_turned(0)
            for q in range(NCH):
                if q + 1 < NCH:
                    keep_turned(q + 1)
                keep_products(q)
            load_experts()

        @block.vector
        def _(dve):
            steps = m.dve_steps(dve)

            def keep_turned(q):
                dve.wait_ge(turned, q + 1)
                if q >= 2:
                    dve.wait_ge(v_made, q - 1)
                dve.tensor_copy(ct[:, q % 2, 1], turn[1][:, :]).then_inc(ct_ready, 1)

            def keep_products(q):
                dve.wait_ge(kt_made, q + 1)
                dve.tensor_copy(kt[:, 1, q * 512:(q + 1) * 512], ktp[1][:, :]).then_inc(kt_kept, 1)
                dve.wait_ge(v_made, q + 1)
                dve.tensor_copy(v[:, q * CH + 2:q * CH + 4], vp[1][:, :].rearrange("p (k n) -> p k n", k=2)).then_inc(v_kept, 1)

            keep_turned(0)
            for q in range(NCH):
                if q + 1 < NCH:
                    keep_turned(q + 1)
                keep_products(q)
            dve.wait_ge(x_in, 32)
            for t in range(T):
                ins = dve.bn_stats(m.stats[:, 0, t], m.x[:, t])
            steps.did(ins)
            steps.wait()
            finish_stats(m, dve, steps, m.stats[:, 0], m.mean[:], m.tmp[:, 3, 0:T], LN_EPS, T).then_inc(var_ready, 1)

        @block.gpsimd
        def _(pool):
            pool.wait_ge(var_ready, 1)
            pool.wait_ge(head_w_in, 32)
            pool.tensor_tensor(m.rstd[:, 0:T], m.tmp[:, 3, 0:T], m.c("neg_half")[:, 0:T], ALU.pow).then_inc(rstd_ready, 1)


def retention_scores_phase(m, a):
    nc = m.nc
    xn_ready, turned = m.sem("xn_ready"), m.sem("xn_turned")
    xt_ready, qt_made, qt_ready = m.sem("xt_ready"), m.sem("qt_made"), m.sem("qt_ready")
    gate_made, gate_kept, scored = m.sem("gate_made"), m.sem("gate_kept"), m.sem("scored")
    masked, a_turned = m.sem("masked"), m.sem("a_turned")

    xn = m.stage[:, 0:2048].rearrange("p (u k d) -> p u k d", u=2, k=CH)
    xt = m.stage[:, 2048:4096].rearrange("p (u c n) -> p u c n", u=2, c=DC)
    qt = m.stage[:, 4096:5120].rearrange("p (h n) -> p h n", h=RH)
    kt = m.rows[:, 0:4096].rearrange("p (h n) -> p h n", h=RH)
    gate = m.rows[:, 8192:12288].rearrange("p (t n) -> p t n", t=T)
    m.at = m.bias[:, 512:768].rearrange("p (h s) -> p h s", h=RH)
    am = m.bias[:, 768:1024].rearrange("p (h s) -> p h s", h=RH)
    ab = m.bias[:, 1024:1280].rearrange("p (h s) -> p h s", h=RH)
    head_w = m.proj[:, 0:RH * P].rearrange("p (h e) -> p h e", h=RH)
    wg_w = m.proj[:, 256:768].rearrange("p (c n) -> p c n", c=DC)
    ident = m.c("ident")
    decay = m.c("decay").rearrange("p (h n) -> p h n", h=RH)
    turn, qp, gp, sp_ = m.ps[0:2], m.ps[2:4], m.ps[4:6], m.ps[6:8]

    with nc.Block() as block:

        @block.tensor
        def _(pe):
            def transposes(q):
                pe.wait_ge(xn_ready, q + 1)
                if q >= 1:
                    pe.wait_ge(xt_ready, 2 * q)
                for c in range(DC):
                    for k in range(CH):
                        mm = pe.transpose(turn[c][:, k * P:(k + 1) * P], xn[:, q % 2, k, c * P:(c + 1) * P], ident)
                mm.then_inc(turned, 1)

            def products(q):
                pe.wait_ge(xt_ready, 2 * (q + 1))
                if q >= 1:
                    pe.wait_ge(qt_ready, 2 * q)
                for h in range(RH):
                    mm = pe.matmul(qp[h][:, :], head_w[:, h], xt[:, q % 2, h], start=True, stop=True)
                mm.then_inc(qt_made, 1)
                if q >= 1:
                    pe.wait_ge(gate_kept, 2 * q)
                for k in range(CH):
                    for c in range(DC):
                        at = (k % 2) * D
                        mm = pe.matmul(gp[k // 2][:, at:at + D], xt[:, q % 2, c, k * P:(k + 1) * P], wg_w[:, c],
                                       start=(c == 0), stop=(c == DC - 1))
                mm.then_inc(gate_made, 1)
                pe.wait_ge(qt_ready, 2 * (q + 1))
                for h in range(RH):
                    for k in range(CH):
                        b = q * CH + k
                        mm = pe.matmul(sp_[h][:, 0:P], qt[:, h, k * P:(k + 1) * P], kt[:, h, b * P:(b + 1) * P],
                                       start=(b == 0), stop=(b == T - 1))
                mm.then_inc(scored, 1)

            pe.wait_ge(m.a_w_in, 64)
            transposes(0)
            for q in range(NCH):
                if q + 1 < NCH:
                    transposes(q + 1)
                products(q)
            pe.wait_ge(masked, 1)
            for h in range(RH):
                mm = pe.transpose(turn[0][:, h * P:(h + 1) * P], am[:, h], ident)
            mm.then_inc(a_turned, 1)

        @block.scalar
        def _(act):
            def keep_turned(q):
                act.wait_ge(turned, q + 1)
                if q >= 2:
                    act.wait_ge(gate_made, q - 1)
                act.copy(xt[:, q % 2, 0], turn[0][:, :]).then_inc(xt_ready, 1)

            keep_turned(0)
            for q in range(NCH):
                if q + 1 < NCH:
                    keep_turned(q + 1)
                act.wait_ge(qt_made, q + 1)
                if q >= 1:
                    act.wait_ge(scored, q)
                act.copy(qt[:, 0], qp[0][:, :]).then_inc(qt_ready, 1)
                act.wait_ge(gate_made, q + 1)
                for g in range(2):
                    at = q * CH + 2 * g
                    act.activation(gate[:, at:at + 2], gp[g][:, :].rearrange("p (k n) -> p k n", k=2),
                                   ACT.Relu).then_inc(gate_kept, 1)

        @block.vector
        def _(dve):
            steps = m.dve_steps(dve)

            def normalise(q):
                if q >= 2:
                    dve.wait_ge(turned, q - 1)
                for k in range(CH):
                    t = q * CH + k
                    ins = dve.tensor_scalar(xn[:, q % 2, k], m.x[:, t], m.mean[:, t:t + 1], m.rstd[:, t:t + 1],
                                            ALU.subtract, ALU.mult)
                ins.then_inc(xn_ready, 1)

            def keep_turned(q):
                dve.wait_ge(turned, q + 1)
                if q >= 2:
                    dve.wait_ge(gate_made, q - 1)
                dve.tensor_copy(xt[:, q % 2, 1], turn[1][:, :]).then_inc(xt_ready, 1)

            dve.wait_ge(m.rstd_ready, 1)
            normalise(0)
            normalise(1)
            keep_turned(0)
            for q in range(NCH):
                if q + 1 < NCH:
                    keep_turned(q + 1)
                if q + 2 < NCH:
                    normalise(q + 2)
                dve.wait_ge(qt_made, q + 1)
                if q >= 1:
                    dve.wait_ge(scored, q)
                dve.tensor_copy(qt[:, 1], qp[1][:, :]).then_inc(qt_ready, 1)
            dve.wait_ge(scored, NCH)
            for h in range(RH):
                ins = dve.tensor_tensor(am[:, h], sp_[h][:, 0:P], decay[:, h], ALU.mult)
            steps.did(ins)
            steps.wait()
            steps.did(dve.scalar_tensor_tensor(ab[:, :, :], am[:, :, :], -1.0, am[:, :, :], ALU.mult, ALU.max))
            steps.wait()
            dve.tensor_scalar(am[:, :, :], ab[:, :, :], 1.0, None, ALU.max).then_inc(masked, 1)
            dve.wait_ge(a_turned, 1)
            steps.did(dve.tensor_copy(m.at, turn[0][:, 0:RH * P].rearrange("p (h s) -> p h s", h=RH)))
            m.at_step = steps.n


def retention_output_phase(m, a):
    nc = m.nc
    made, kept = m.sem("o_made"), [m.sem(f"o_kept{u}") for u in range(2)]
    var_ready, rstd_ready = m.sem("gn_var_ready"), m.sem("gn_rstd_ready")
    m.gn_rstd_ready = rstd_ready
    v = m.rows[:, 4096:8192].rearrange("p (t h e) -> p t h e", t=T, h=RH)
    o = m.rows[:, 0:4096].rearrange("p (t n) -> p t n", t=T)
    op = m.ps[0:2]

    with nc.Block() as block:

        @block.tensor
        def _(pe):
            pe.wait_ge(m.dve_chain, m.at_step)
            for j in rounds(pe, 0, T // 4):
                for u in range(2):
                    pe.wait_ge(kept[u], j)
                    for h in range(RH):
                        out = op[u][:, :].rearrange("p (k h e) -> p k h e", k=2, h=RH)[:, :, h]
                        mm = pe.matmul(out, m.at[:, h], v[:, bass.ds(j * 4 + 2 * u, 2), h], start=True, stop=True)
                    mm.then_inc(made, 1)

        @block.scalar
        def _(act):
            for j in rounds(act, 0, T // 4):
                for u in range(2):
                    act.wait_ge(made, j * 2 + (u + 1))
                    act.copy(o[:, bass.ds(j * 4 + 2 * u, 2)], op[u][:, :].rearrange("p (k n) -> p k n", k=2)).then_inc(kept[u], 1)

        @block.vector
        def _(dve):
            steps = m.dve_steps(dve)
            base = steps.n
            for j in rounds(dve, 0, T // 4):
                steps.n = base + j * 4
                for u in range(2):
                    dve.wait_ge(kept[u], j + 1)
                    for k in range(2):
                        t = j * 4 + (2 * u + k)
                        steps.did(dve.bn_stats(m.stats[:, 0, bass.ds(t, 1)].rearrange("p a n -> p (a n)"),
                                               o[:, bass.ds(t, 1)].rearrange("p a n -> p (a n)")))
            steps.n = base + T
            steps.wait()
            finish_stats(m, dve, steps, m.stats[:, 0], m.mean[:], m.tmp[:, 3, 0:T], GN_EPS, T).then_inc(var_ready, 1)

        @block.gpsimd
        def _(pool):
            pool.wait_ge(var_ready, 1)
            pool.tensor_tensor(m.rstd[:, 0:T], m.tmp[:, 3, 0:T], m.c("neg_half")[:, 0:T], ALU.pow).then_inc(rstd_ready, 1)


def tile(ap, t):
    return ap[:, bass.ds(t, 1)].rearrange("p a n -> p (a n)")


def col(ap, t):
    return ap[:, bass.ds(t, 1)]


def retention_close_phase(m, a):
    nc = m.nc
    y_norm, y_gated = [[m.sem(f"{n}{u}") for u in range(2)] for n in ("y_norm", "y_gated")]
    y_turned, yt_ready, y_out, x_added = [[m.sem(f"{n}{u}") for u in range(2)] for n in
                                          ("y_turned", "yt_ready", "y_out", "x_added0_")]
    var_ready, rstd_ready = m.sem("ln1_var_ready"), m.sem("ln1_rstd_ready")
    m.ln1_rstd_ready = rstd_ready
    o = m.rows[:, 0:4096].rearrange("p (t n) -> p t n", t=T)
    gate = m.rows[:, 8192:12288].rearrange("p (t n) -> p t n", t=T)
    wo_w = m.proj[:, 768:1280].rearrange("p (c n) -> p c n", c=DC)
    gamma, beta = m.bias[:, 0:D], m.bias[:, D:2 * D]
    y = m.stage[:, 0:512].rearrange("p (u n) -> p u n", u=2)
    z = m.stage[:, 512:1024].rearrange("p (u n) -> p u n", u=2)
    yt = m.stage[:, 1024:1536].rearrange("p (u c n) -> p u c n", u=2, c=DC)
    ident = m.c("ident")
    turn, out = m.ps[0:2], m.ps[2:4]

    with nc.Block() as block:

        @block.vector
        def _(dve):
            steps = m.dve_steps(dve)
            dve.wait_ge(m.gn_rstd_ready, 1)

            def gated(j, u):
                t = j * 2 + u
                dve.wait_ge(y_turned[u], j)
                steps.did(dve.tensor_scalar(y[:, u], tile(o, t), col(m.mean, t), col(m.rstd, t), ALU.subtract, ALU.mult))
                steps.wait()
                steps.did(dve.tensor_tensor(z[:, u], y[:, u], gamma, ALU.mult))
                steps.wait()
                steps.did(dve.tensor_tensor(y[:, u], z[:, u], beta, ALU.add))
                steps.wait()
                dve.tensor_tensor(z[:, u], y[:, u], tile(gate, t), ALU.mult).then_inc(y_gated[u], 1)

            def add(j, u):
                t = j * 2 + u
                dve.wait_ge(y_out[u], j + 1)
                dve.tensor_tensor(tile(m.x, t), tile(m.x, t), out[u][:, 0:D], ALU.add).then_inc(x_added[u], 1)

            def stats(j, u):
                t = j * 2 + u
                dve.wait_ge(x_added[u], j + 1)
                steps.did(dve.bn_stats(tile(m.stats[:, 0], t), tile(m.x, t)))

            base = steps.n
            gated(0, 0)
            gated(0, 1)
            for j in rounds(dve, 0, T // 2 - 1):
                steps.n = base + 6 + j * 8
                for u in range(2):
                    add(j, u)
                    gated(j + 1, u)
                    stats(j, u)
            steps.n = base + 6 + (T // 2 - 1) * 8
            for u in range(2):
                add(T // 2 - 1, u)
                stats(T // 2 - 1, u)
            steps.wait()
            finish_stats(m, dve, steps, m.stats[:, 0], m.mean[:], m.tmp[:, 3, 0:T], LN_EPS, T).then_inc(var_ready, 1)

        @block.tensor
        def _(pe):
            for j in rounds(pe, 0, T // 2):
                for u in range(2):
                    pe.wait_ge(y_gated[u], j + 1)
                    pe.wait_ge(yt_ready[u], j)
                    for c in range(DC):
                        mm = pe.transpose(turn[u][:, c * P:(c + 1) * P], z[:, u, c * P:(c + 1) * P], ident)
                    mm.then_inc(y_turned[u], 1)
                for u in range(2):
                    pe.wait_ge(yt_ready[u], j + 1)
                    pe.wait_ge(x_added[u], j)
                    for c in range(DC):
                        mm = pe.matmul(out[u][:, 0:D], yt[:, u, c], wo_w[:, c], start=(c == 0), stop=(c == DC - 1))
                    mm.then_inc(y_out[u], 1)

        @block.scalar
        def _(act):
            for j in rounds(act, 0, T // 2):
                for u in range(2):
                    act.wait_ge(y_turned[u], j + 1)
                    act.wait_ge(y_out[u], j)
                    act.copy(yt[:, u], turn[u][:, 0:D].rearrange("p (c n) -> p c n", c=DC)).then_inc(yt_ready[u], 1)

        @block.gpsimd
        def _(pool):
            pool.wait_ge(var_ready, 1)
            pool.tensor_tensor(m.rstd[:, 0:T], m.tmp[:, 3, 0:T], m.c("neg_half")[:, 0:T], ALU.pow).then_inc(rstd_ready, 1)


class Layer:

    def __init__(self, n):
        self.n, self.e, self.k, self.nb = n, (E0, E1)[n], (K0, K1)[n], (NB0, NB1)[n]
        self.cols = max(self.e, 8)


def logits_phase(m, a, n):
    nc, L = m.nc, Layer(n)
    sem = lambda name: [m.sem(f"{name}{n}_{u}") for u in range(4)]
    xn_ready, xn_turned, xn_stored = sem("rx_ready"), sem("rx_turned"), sem("rx_stored")
    xt_ready, logit_made, logit_kept = sem("rxt_ready"), sem("logit_made"), sem("logit_kept")
    xn = m.stage[:, 0:1024].rearrange("p (u n) -> p u n", u=4)
    xt = m.stage[:, 1024:2048].rearrange("p (u c n) -> p u c n", u=4, c=DC)
    m.logits = m.rows[:, 0:T * L.cols].rearrange("p (t e) -> p t e", t=T)
    router = (m.router0, m.router1)[n]
    rbias = (m.rbias0, m.rbias1)[n]
    ident = m.c("ident")
    turn, lg = m.ps[0:4], m.ps[4:8]
    xn_rows = a[f"xn{n}"].rearrange("(t p) d -> p t d", p=P)
    turns = T // 4

    with nc.Block() as block:

        @block.vector
        def _(dve):
            steps = m.dve_steps(dve)
            dve.wait_ge(m.ln3_rstd_ready if n else m.ln1_rstd_ready, 1)
            if L.cols > L.e:
                steps.did(dve.memset(m.logits[:, :, L.e:], -3e38))

            def normalise(j, u):
                t = j * 4 + u
                dve.wait_ge(xn_turned[u], j)
                dve.wait_ge(xn_stored[u], j * 16)
                dve.tensor_scalar(xn[:, u], tile(m.x, t), col(m.mean, t), col(m.rstd, t),
                                  ALU.subtract, ALU.mult).then_inc(xn_ready[u], 1)

            def keep(j, u):
                dve.wait_ge(logit_made[u], j + 1)
                dve.tensor_tensor(tile(m.logits, j * 4 + u)[:, 0:L.e], lg[u][:, 0:L.e], rbias[:], ALU.add).then_inc(logit_kept[u], 1)

            for u in range(4):
                normalise(0, u)
            for j in rounds(dve, 0, turns - 1):
                for u in range(4):
                    keep(j, u)
                    normalise(j + 1, u)
            for u in range(4):
                keep(turns - 1, u)

        @block.tensor
        def _(pe):
            if n == 0:
                pe.wait_ge(m.late_in, 64)

            for j in rounds(pe, 0, turns):
                for u in range(4):
                    pe.wait_ge(xn_ready[u], j + 1)
                    pe.wait_ge(xt_ready[u], j)
                    for c in range(DC):
                        mm = pe.transpose(turn[u][:, c * P:(c + 1) * P], xn[:, u, c * P:(c + 1) * P], ident)
                    mm.then_inc(xn_turned[u], 1)
                for u in range(4):
                    pe.wait_ge(xt_ready[u], j + 1)
                    pe.wait_ge(logit_kept[u], j)
                    for c in range(DC):
                        mm = pe.matmul(lg[u][:, 0:L.e], xt[:, u, c], router[:, c], start=(c == 0), stop=(c == DC - 1))
                    mm.then_inc(logit_made[u], 1)

        @block.scalar
        def _(act):
            if n == 1:
                for e in range(E1):
                    act.dma_start(m.weights[:, 16384 + e * 512:16384 + (e + 1) * 512].rearrange("p (c n) -> p c n", c=DC),
                                  a["L1_ffn_down_proj"][e].rearrange("(c p) n -> p c n", c=DC)).then_inc(m.w1_in, 16)
            for j in rounds(act, 0, turns):
                for u in range(4):
                    act.wait_ge(xn_turned[u], j + 1)
                    act.wait_ge(logit_made[u], j)
                    act.copy(xt[:, u], turn[u][:, 0:D].rearrange("p (c n) -> p c n", c=DC)).then_inc(xt_ready[u], 1)

        @block.sync
        def _(sp):
            for j in rounds(sp, 0, turns):
                for u in range(4):
                    sp.wait_ge(xn_ready[u], j + 1)
                    sp.dma_start(xn_rows[:, bass.ds(j * 4 + u, 1)].rearrange("p a n -> p (a n)"), xn[:, u]).then_inc(xn_stored[u], 16)
            for u in range(4):
                sp.wait_ge(xn_stored[u], 16 * turns)


def routing_phase(m, a, n):
    nc, L = m.nc, Layer(n)
    E, K, NB = L.e, L.k, L.nb
    shifted, exped = m.sem(f"shifted{n}"), m.sem(f"exped{n}")
    hot_ready, counted = m.sem(f"hot_ready{n}"), m.sem(f"counted{n}")
    entry_ready, entry_used = [[m.sem(f"{s}{n}_{u}") for u in range(4)] for s in ("entry_ready", "entry_used")]
    table_made = m.sem(f"table_made{n}")

    cursor = [T * L.cols]

    def take(size, dt=F32):
        at = cursor[0]
        cursor[0] += size
        return m.rows[:, at:at + size].bitcast(dt) if dt != F32 else m.rows[:, at:at + size]

    top = take(8 * T).rearrange("p (t k) -> p t k", t=T)
    top_at = take(8 * T, U32).rearrange("p (t k) -> p t k", t=T)
    top_atf = take(8 * T).rearrange("p (t k) -> p t k", t=T)
    wide = E if K == 1 else K
    ex = take(wide * T).rearrange("p (t k) -> p t k", t=T)
    exs = take(T)
    hot = [take(E * T).rearrange("p (e t) -> p e t", e=E) for _ in range(K)]
    hots = hot[0] if K == 1 else take(E * T).rearrange("p (e t) -> p e t", e=E)
    hots2 = take(E * T).rearrange("p (e t) -> p e t", e=E)
    count = take(E * T).rearrange("p (e t) -> p e t", e=E)
    upto = take(E * T).rearrange("p (e t) -> p e t", e=E)
    place = take(E * T).rearrange("p (e t) -> p e t", e=E)
    work = [take(E * T).rearrange("p (e t) -> p e t", e=E) for _ in range(K)]
    blocks, blocks_to, first = take(E), take(E), take(E)
    pos = take(K * T)
    posi, blki = take(K * T, I32), take(K * T, I32)
    blk, row = take(K * T), take(K * T)
    owner = take(NB * E).rearrange("p (b e) -> p b e", b=NB)
    ownf, ownc = take(NB), take(NB)
    tb, gap, tb2 = take(NB), take(NB), take(NB)
    srci = take(NB, I32)
    assert cursor[0] <= 12416
    row_hot = m.stage[:, 0:4 * P].rearrange("p (u s) -> p u s", u=4)
    value = m.stage[:, 512:512 + 4 * NB].rearrange("p (u b) -> p u b", u=4)
    psum_rank, psum_count = m.ps[0][:, 0:E * T], m.ps[1][:, 0:E * T]
    table = m.ps[2][:, 0:NB]
    dest_token = m.c(f"dest{n}")
    entries = K * T // 4

    with nc.Block() as block:

        @block.vector
        def _(dve):
            steps = m.dve_steps(dve)
            did, wait = steps.did, steps.wait
            for t in range(T):
                ins = dve.max(top[:, t], m.logits[:, t])
            did(ins)
            wait()
            for t in range(T):
                ins = dve.max_index(top_at[:, t], top[:, t], m.logits[:, t])
            did(ins)
            best = top[:, :, 0:1].to_broadcast([P, T, wide])
            dve.tensor_tensor(ex, m.logits[:, :, 0:E] if K == 1 else top[:, :, 0:K], best, ALU.subtract).then_inc(shifted, 1)
            wait()
            did(dve.tensor_copy(top_atf, top_at))
            wait()
            experts = m.c("expert")[:, 0:E * T].rearrange("p (e t) -> p e t", e=E)
            for k in range(K):
                ins = dve.tensor_tensor(hot[k], experts, top_atf[:, :, k].unsqueeze(1).to_broadcast([P, E, T]), ALU.is_equal)
            did(ins)
            wait()
            if K == 1:
                dve.sem_inc(hot_ready, 1)
            else:
                did(dve.tensor_tensor(hots2, hot[0], hot[1], ALU.add))
                did(dve.tensor_tensor(place, hot[2], hot[3], ALU.add))
                wait()
                dve.tensor_tensor(hots, hots2, place, ALU.add).then_inc(hot_ready, 1)
            dve.wait_ge(exped, 1)
            did(dve.tensor_reduce(exs, ex, X_AXIS, ALU.add))
            wait()
            if K == 1:
                did(dve.reciprocal(m.pick_w[:, 0], exs))
            else:
                did(dve.reciprocal(exs, exs))
                wait()
                did(dve.tensor_tensor(m.pick_w[:, 0:K].rearrange("p k t -> p t k"), ex,
                                      exs.unsqueeze(2).to_broadcast([P, T, K]), ALU.mult))
            dve.wait_ge(counted, 1)
            did(dve.tensor_copy(count, psum_count.rearrange("p (e t) -> p e t", e=E)))
            wait()
            flat = lambda ap: ap.rearrange("p e t -> p (e t)")
            did(dve.tensor_tensor_scan(flat(upto), m.c("carry")[:, 0:E * T], flat(count), 0.0, ALU.mult, ALU.add))
            wait()
            did(dve.tensor_tensor(work[0], m.c("full")[:, 0:E * T].rearrange("p (e t) -> p e t", e=E),
                                  upto[:, :, T - 1:T].to_broadcast([P, E, T]), ALU.is_lt))
            did(dve.tensor_tensor(place, upto, count, ALU.subtract))
            wait()
            did(dve.tensor_reduce(blocks, work[0], X_AXIS, ALU.add))
            did(dve.tensor_tensor(hots2, place, psum_rank.rearrange("p (e t) -> p e t", e=E), ALU.add))
            wait()
            did(dve.tensor_tensor_scan(blocks_to, m.c("ones")[:, 0:E], blocks, 0.0, ALU.mult, ALU.add))
            wait()
            did(dve.tensor_tensor(first, blocks_to, blocks, ALU.subtract))
            did(dve.tensor_tensor(owner[0:1], blocks_to[0:1].unsqueeze(1).to_broadcast([1, NB, E]),
                                  m.c("iota")[0:1, 0:NB].unsqueeze(2).to_broadcast([1, NB, E]), ALU.is_le))
            wait()
            did(dve.scalar_tensor_tensor(place, first.unsqueeze(2).to_broadcast([P, E, T]), float(P), hots2, ALU.mult, ALU.add))
            did(dve.tensor_reduce(ownf[0:1], owner[0:1], X_AXIS, ALU.add))
            wait()
            for k in range(K):
                ins = dve.tensor_tensor(work[k], hot[k], place, ALU.mult)
            did(ins)
            did(dve.tensor_scalar(m.block_expert[:, 0:NB], ownf[0:1], float(E - 1), None, ALU.min))
            wait()
            for k in range(K):
                ins = dve.tensor_reduce(pos[:, k * T:(k + 1) * T], work[k].rearrange("p e t -> p t e"), X_AXIS, ALU.add)
            did(ins)
            wait()
            did(dve.tensor_copy(posi, pos))
            wait()
            did(dve.tensor_single_scalar(blki, posi, 7, ALU.arith_shift_right))
            wait()
            did(dve.tensor_copy(blk, blki))
            wait()
            did(dve.scalar_tensor_tensor(row, blk, -float(P), pos, ALU.mult, ALU.add))
            wait()

            def entry(j, u):
                i = j * 4 + u
                dve.wait_ge(entry_used[u], j)
                did(dve.tensor_scalar(row_hot[:, u], m.c("iota"), col(row, i), None, ALU.is_equal))
                dve.tensor_scalar(value[:, u], m.c("iota")[:, 0:NB], col(blk, i), col(dest_token, i),
                                  ALU.is_equal, ALU.mult).then_inc(entry_ready[u], 1)

            base = steps.n
            for j in rounds(dve, 0, entries):
                steps.n = base + j * 4
                for u in range(4):
                    entry(j, u)
            steps.n = base + entries * 4
            dve.wait_ge(table_made, 1)
            did(dve.tensor_scalar(gap, table, 0.5, None, ALU.is_lt))
            did(dve.tensor_scalar(tb, table, -1.0, None, ALU.add))
            wait()
            did(dve.tensor_tensor(gap, gap, m.c(f"trash{n}"), ALU.mult))
            did(dve.tensor_scalar(srci, tb, 0.0, None, ALU.max))
            wait()
            did(dve.tensor_tensor(m.dest[:, 0:NB], gap, tb, ALU.add))
            did(dve.tensor_single_scalar(m.source[:, 0:NB], srci, K.bit_length() - 1, ALU.arith_shift_right))

        @block.scalar
        def _(act):
            act.wait_ge(shifted, 1)
            act.activation(ex, ex, ACT.Exp).then_inc(exped, 1)

        @block.tensor
        def _(pe):
            pe.wait_ge(hot_ready, 1)
            flat = hots.rearrange("p e t -> p (e t)")
            pe.matmul(psum_rank, m.c("before"), flat, start=True, stop=True)
            pe.matmul(psum_count, m.c("ones"), flat, start=True, stop=True).then_inc(counted, 1)

            def entry(j, u, start=False, stop=False):
                pe.wait_ge(entry_ready[u], j + 1)
                return pe.matmul(table, row_hot[:, u], value[:, u], start=start, stop=stop)

            for u in range(4):
                entry(0, u, start=(u == 0)).then_inc(entry_used[u], 1)
            for j in rounds(pe, 1, entries - 1):
                for u in range(4):
                    entry(j, u).then_inc(entry_used[u], 1)
            for u in range(4):
                mm = entry(entries - 1, u, stop=(u == 3))
            mm.then_inc(table_made, 1)


def gather_and_scatter(m, pool, a, n, rows_in, rows_in_sem, rows_taken, out, out_ready, stored, nb, bufs, lag):
    for b in range(nb + lag):
        if b < nb:
            i = b % bufs
            if b >= bufs:
                pool.wait_ge(rows_taken[i], b // bufs)
            pool.indirect_dma_start(rows_in[:, i], None, a[f"xn{n}"],
                                    bass.IndirectOffsetOnAxis(ap=m.source[:, b:b + 1], axis=0)).then_inc(rows_in_sem[i], 16)
        d = b - lag
        if d >= 0:
            i = d % bufs
            pool.wait_ge(out_ready[i], d // bufs + 1)
            pool.indirect_dma_start(a[f"y{n}"], bass.IndirectOffsetOnAxis(ap=m.dest[:, d:d + 1], axis=0),
                                    out[:, i], None).then_inc(stored[i], 16)
    for i in range(bufs):
        pool.wait_ge(stored[i], 16 * ((nb - i + bufs - 1) // bufs))


def experts0_phase(m, a):
    nc = m.nc
    NB, FH = NB0, F0 // 2
    FC = FH // P
    sem = m.sem
    BUFS = 1
    rows_in = [sem(f"e0_in{i}") for i in range(BUFS)]
    stored = [sem(f"e0_stored{i}") for i in range(BUFS)]
    turned, xt_ready = sem("e0_turned"), sem("e0_xt_ready")
    gu_made, sig_ready, h_ready = [[sem(f"{s}{u}") for u in range(2)] for s in ("e0_gu", "e0_sig", "e0_h")]
    h_turned, ht_ready, down_made = [[sem(f"{s}{u}") for u in range(2)] for s in ("e0_ht", "e0_htr", "e0_down")]
    y_ready = sem("e0_y_ready")
    m.c_w_in = m.lasting("c_w_in")
    part = m.rows[:, 0:4096]
    xg = m.stage[:, 0:256].rearrange("p (u n) -> p u n", u=1)
    xt = m.stage[:, 256:512].rearrange("p (c n) -> p c n", c=DC)
    yo = m.stage[:, 512:768].rearrange("p (u n) -> p u n", u=1)
    sig = part[:, 0:1024].rearrange("p (u n) -> p u n", u=2)
    prod = part[:, 1024:2048].rearrange("p (u n) -> p u n", u=2)
    hid = part[:, 2048:3072].rearrange("p (u n) -> p u n", u=2)
    ht = part[:, 3072:4096].rearrange("p (u c n) -> p u c n", u=2, c=FC)
    g_ps = [m.ps[0], m.ps[2]]
    u_ps = [m.ps[1], m.ps[3]]
    x_turn, h_turn, y_ps = m.ps[4], m.ps[5], m.ps[6]
    ident = m.c("ident")
    wg = m.weights[:, 0:8192].rearrange("p (e c f) -> p e c f", e=E0, c=DC)
    wu = m.weights[:, 8192:16384].rearrange("p (e c f) -> p e c f", e=E0, c=DC)
    wd = m.weights[:, 16384:24576].rearrange("p (e c n) -> p e c n", e=E0, c=F0 // P)

    with nc.Block() as block:

        @block.gpsimd
        def _(pool):
            gather_and_scatter(m, pool, a, 0, xg, rows_in, [turned], yo, [y_ready], stored, NB, BUFS, 2)

        @block.sync
        def _(sp):
            for i, w in enumerate(("Wq", "Wk_img", "Wv_img", "Wo")):
                sp.dma_start(m.proj[:, i * 512:(i + 1) * 512].rearrange("p (c n) -> p c n", c=DC),
                             a[f"L1_xattn_{w}"].rearrange("(c p) n -> p c n", c=DC)).then_inc(m.c_w_in, 16)
            for i, w in enumerate(("bq", "bk_img", "gq", "gk_img", "bv_img", "bo")):
                sp.dma_start(m.bias[:, i * D:(i + 1) * D], a[f"L1_xattn_{w}"].partition_broadcast(P)).then_inc(m.c_w_in, 16)

        @block.tensor
        def _(pe):
            def turn_rows(b):
                pe.wait_ge(rows_in[0], 16 * (b + 1))
                pe.wait_ge(xt_ready, b)
                for c in range(DC):
                    mm = pe.transpose(x_turn[:, c * P:(c + 1) * P], xg[:, 0, c * P:(c + 1) * P], ident)
                mm.then_inc(turned, 1)

            def gate_up(b, e, u):
                if u == 0:
                    pe.wait_ge(xt_ready, b + 1)
                pe.wait_ge(h_ready[u], b)
                for w, ps in ((wg, g_ps[u]), (wu, u_ps[u])):
                    for c in range(DC):
                        rhs = w[:, bass.ds(e, 1), c, u * FH:(u + 1) * FH].rearrange("p a f -> p (a f)")
                        mm = pe.matmul(ps[:, :], xt[:, c], rhs, start=(c == 0), stop=(c == DC - 1))
                mm.then_inc(gu_made[u], 1)

            def turn_hidden(b, u):
                pe.wait_ge(h_ready[u], b + 1)
                if u == 0:
                    pe.wait_ge(ht_ready[1], b)
                else:
                    pe.wait_ge(ht_ready[0], b + 1)
                for c in range(FC):
                    mm = pe.transpose(h_turn[:, c * P:(c + 1) * P], hid[:, u, c * P:(c + 1) * P], ident)
                mm.then_inc(h_turned[u], 1)

            def down(b, e, u):
                pe.wait_ge(ht_ready[u], b + 1)
                if u == 0:
                    pe.wait_ge(y_ready, b)
                for c in range(FC):
                    rhs = wd[:, bass.ds(e, 1), u * FC + c].rearrange("p a n -> p (a n)")
                    mm = pe.matmul(y_ps[:, 0:D], ht[:, u, c], rhs, start=(u == 0 and c == 0), stop=(u == 1 and c == FC - 1))
                mm.then_inc(down_made[u], 1)

            def expert(b):
                return pe.value_load(m.block_expert[0:1, bass.ds(b, 1)], min_val=0, max_val=E0 - 1)

            def step(b, last=False):
                e, e_before = expert(b), expert(b - 1)
                turn_hidden(b - 1, 0)
                gate_up(b, e, 0)
                down(b - 1, e_before, 0)
                turn_hidden(b - 1, 1)
                gate_up(b, e, 1)
                if not last:
                    turn_rows(b + 1)
                down(b - 1, e_before, 1)

            pe.wait_ge(m.w0_in, 16 * 3 * E0)
            turn_rows(0)
            e = expert(0)
            gate_up(0, e, 0)
            gate_up(0, e, 1)
            turn_rows(1)
            for b in rounds(pe, 1, NB - 1):
                step(b)
            step(NB - 1, last=True)
            e = expert(NB - 1)
            for u in range(2):
                turn_hidden(NB - 1, u)
                down(NB - 1, e, u)

        @block.scalar
        def _(act):
            def sigmoid(b, u):
                act.wait_ge(gu_made[u], b + 1)
                act.activation(sig[:, u], g_ps[u][:, :], ACT.Sigmoid).then_inc(sig_ready[u], 1)

            def keep_hidden(b, u):
                act.wait_ge(h_turned[u], b + 1)
                act.copy(ht[:, u], h_turn[:, :].rearrange("p (c n) -> p c n", c=FC)).then_inc(ht_ready[u], 1)

            def keep_rows(b):
                act.wait_ge(turned, b + 1)
                act.wait_ge(gu_made[1], b)
                act.copy(xt[:, :], x_turn[:, 0:D].rearrange("p (c n) -> p c n", c=DC)).then_inc(xt_ready, 1)

            def keep_out(b):
                act.wait_ge(down_made[1], b + 1)
                act.wait_ge(stored[0], b * 16)
                act.copy(yo[:, 0], y_ps[:, 0:D]).then_inc(y_ready, 1)

            keep_rows(0)
            sigmoid(0, 0)
            sigmoid(0, 1)
            keep_rows(1)

            def step(b, last=False):
                keep_hidden(b - 1, 0)
                sigmoid(b, 0)
                keep_hidden(b - 1, 1)
                sigmoid(b, 1)
                if not last:
                    keep_rows(b + 1)
                keep_out(b - 1)

            for b in rounds(act, 1, NB - 1):
                step(b)
            step(NB - 1, last=True)
            keep_hidden(NB - 1, 0)
            keep_hidden(NB - 1, 1)
            keep_out(NB - 1)

        @block.vector
        def _(dve):
            steps = m.dve_steps(dve)
            base = steps.n
            for b in rounds(dve, 0, NB):
                steps.n = base + b * 2
                for u in range(2):
                    dve.wait_ge(sig_ready[u], b + 1)
                    steps.did(dve.tensor_tensor(prod[:, u], g_ps[u][:, :], sig[:, u], ALU.mult))
                    steps.wait()
                    dve.wait_ge(h_turned[u], b)
                    dve.tensor_tensor(hid[:, u], u_ps[u][:, :], prod[:, u], ALU.mult).then_inc(h_ready[u], 1)
            steps.n = base + NB * 2


def combine_phase(m, a, n):
    nc, L = m.nc, Layer(n)
    K = L.k
    sem = lambda name: [m.sem(f"{name}{n}_{u}") for u in range(4)]
    y_in, x_ready, out_done = sem("y_in"), sem("xc_ready"), sem("out_done")
    var_ready = m.sem(f"c_var_ready{n}")
    if n == 0:
        m.ln2_rstd_ready = m.lasting("ln2_rstd_ready")
        m.w1_in = m.lasting("w1_in")
    y = m.stage[:, 0:4 * K * D].rearrange("p (u k d) -> p u k d", u=4, k=K)
    y_rows = a[f"y{n}"][0:TOKENS * K].rearrange("(t p k) d -> p t (k d)", p=P, k=K)
    out_rows = a["out"].rearrange("(t p) d -> p t d", p=P)
    turns = T // 4

    with nc.Block() as block:

        @block.sync
        def _(sp):
            for j in rounds(sp, 0, turns):
                for u in range(4):
                    sp.wait_ge(x_ready[u], j)
                    sp.dma_start(y[:, u].rearrange("p k d -> p (k d)"),
                                 y_rows[:, bass.ds(j * 4 + u, 1)].rearrange("p a n -> p (a n)")).then_inc(y_in[u], 16)

        @block.vector
        def _(dve):
            steps = m.dve_steps(dve)
            base = steps.n
            per = 4 * (K - 1) + (4 if n == 0 else 0)
            for j in rounds(dve, 0, turns):
                steps.n = base + j * per
                for k in range(K):
                    for u in range(4):
                        t = j * 4 + u
                        if k == 0:
                            dve.wait_ge(y_in[u], j * 16 + 16)
                        else:
                            steps.wait(base + j * per + ((k - 1) * 4 + u + 1))
                        ins = dve.scalar_tensor_tensor(tile(m.x, t), y[:, u, k], col(m.pick_w[:, k], t), tile(m.x, t),
                                                       ALU.mult, ALU.add)
                        if k == K - 1:
                            ins.then_inc(x_ready[u], 1)
                        else:
                            steps.did(ins)
                if n == 0:
                    for u in range(4):
                        t = j * 4 + u
                        dve.wait_ge(x_ready[u], j + 1)
                        steps.did(dve.bn_stats(tile(m.stats[:, 0], t), tile(m.x, t)))
            steps.n = base + turns * per
            if n == 0:
                steps.wait()
                finish_stats(m, dve, steps, m.stats[:, 0], m.mean[:], m.tmp[:, 3, 0:T], LN_EPS, T).then_inc(var_ready, 1)

        if n == 0:
            @block.gpsimd
            def _(pool):
                pool.wait_ge(var_ready, 1)
                pool.tensor_tensor(m.rstd[:, 0:T], m.tmp[:, 3, 0:T], m.c("neg_half")[:, 0:T], ALU.pow).then_inc(m.ln2_rstd_ready, 1)

        @block.scalar
        def _(act):
            if n == 0:
                for u in range(4):
                    act.wait_ge(y_in[u], 16 * turns)
                for e in range(E1):
                    act.dma_start(m.weights[:, e * 1024:(e + 1) * 1024].rearrange("p (c f) -> p c f", c=DC),
                                  a["L1_ffn_gate_up_proj"][e].rearrange("(c p) f -> p c f", c=DC)).then_inc(m.w1_in, 16)
            else:
                for j in rounds(act, 0, turns):
                    for u in range(4):
                        act.wait_ge(x_ready[u], j + 1)
                        act.dma_start(out_rows[:, bass.ds(j * 4 + u, 1)].rearrange("p a n -> p (a n)"),
                                      tile(m.x, j * 4 + u)).then_inc(out_done[u], 16)
                for u in range(4):
                    act.wait_ge(out_done[u], 16 * turns)


def projections_phase(m, a):
    nc, sem = m.nc, m.sem
    ctx_in = [sem(f"c_ctx_in{u}") for u in range(2)]
    xn_ready, turned, xt_ready = sem("c_xn_ready"), sem("c_turned"), sem("c_xt_ready")
    qk_made, v_made, qk_kept, v_kept = sem("qk_made"), sem("v_made1"), sem("qk_kept"), sem("v_kept1")
    biased = sem("bo_added")
    var_ready = sem("rms_var_ready")
    m.rms_ready = sem("rms_ready")
    xn = m.stage[:, 0:512].rearrange("p (u n) -> p u n", u=2)
    cx = m.stage[:, 512:1024].rearrange("p (u n) -> p u n", u=2)
    xct = m.stage[:, 1024:2048].rearrange("p (u w c n) -> p u w c n", u=2, w=2, c=DC)
    qk = m.rows[:, 0:8192].rearrange("p (t n) -> p t n", t=T)
    v = m.rows[:, 8192:12288].rearrange("p (t n) -> p t n", t=T)
    wq, wk, wv = (m.proj[:, i * 512:(i + 1) * 512].rearrange("p (c n) -> p c n", c=DC) for i in range(3))
    bqk, bv, bo = m.bias[:, 0:2 * D], m.bias[:, 4 * D:5 * D], m.bias[:, 5 * D:6 * D]
    turn, qkp, vp = m.ps[0:2], m.ps[2:4], m.ps[4:6]
    ident = m.c("ident")
    ctx_rows = a["ctx_2048"].rearrange("(t p) d -> p t d", p=P)

    with nc.Block() as block:

        @block.sync
        def _(sp):
            for j in rounds(sp, 0, T // 2):
                for u in range(2):
                    t = j * 2 + u
                    if not isinstance(j, int):
                        sp.wait_ge(turned, t - 1)
                    sp.dma_start(cx[:, u], ctx_rows[:, bass.ds(t, 1)].rearrange("p a n -> p (a n)")).then_inc(ctx_in[u], 16)

        @block.vector
        def _(dve):
            steps = m.dve_steps(dve)
            dve.wait_ge(m.ln2_rstd_ready, 1)
            dve.wait_ge(m.c_w_in, 160)

            def normalise(t, u):
                dve.tensor_scalar(xn[:, u], tile(m.x, t), col(m.mean, t), col(m.rstd, t),
                                  ALU.subtract, ALU.mult).then_inc(xn_ready, 1)

            def keep(t, u):
                dve.wait_ge(qk_made, t + 1)
                dve.tensor_tensor(tile(qk, t), qkp[u][:, :], bqk, ALU.add).then_inc(qk_kept, 1)
                dve.wait_ge(v_made, t + 1)
                dve.tensor_tensor(tile(v, t), vp[u][:, 0:D], bv, ALU.add).then_inc(v_kept, 1)
                dve.wait_ge(qk_kept, t + 1)
                for w in range(2):
                    steps.did(dve.bn_stats(tile(m.stats[:, w], t), tile(qk, t)[:, w * D:(w + 1) * D]))

            normalise(0, 0)
            normalise(1, 1)
            base = steps.n
            for j in rounds(dve, 0, T // 2 - 1):
                steps.n = base + j * 4
                for u in range(2):
                    t = j * 2 + u
                    dve.wait_ge(turned, t + 1)
                    normalise(t + 2, u)
                    keep(t, u)
            steps.n = base + (T // 2 - 1) * 4
            for u in range(2):
                keep(T - 2 + u, u)
            steps.wait()
            finish_stats(m, dve, steps, m.stats[:, :].rearrange("p w t s -> p (w t) s"), None, m.tmp[:, 3],
                         RMS_EPS, 2 * T).then_inc(var_ready, 1)

        @block.tensor
        def _(pe):
            def turn_tile(j, t, u):
                pe.wait_ge(xn_ready, t + 1)
                pe.wait_ge(ctx_in[u], j * 16 + 16)
                if not isinstance(t, int) or t >= 2:
                    pe.wait_ge(xt_ready, t - 1)
                for w, src in enumerate((xn, cx)):
                    for c in range(DC):
                        at = (w * DC + c) * P
                        mm = pe.transpose(turn[u][:, at:at + P], src[:, u, c * P:(c + 1) * P], ident)
                mm.then_inc(turned, 1)

            def products(t, u):
                pe.wait_ge(xt_ready, t + 1)
                if not isinstance(t, int) or t >= 2:
                    pe.wait_ge(v_kept, t - 1)
                for w, (src, wt) in enumerate(((0, wq), (1, wk))):
                    for c in range(DC):
                        mm = pe.matmul(qkp[u][:, w * D:(w + 1) * D], xct[:, u, src, c], wt[:, c], start=(c == 0), stop=(c == DC - 1))
                mm.then_inc(qk_made, 1)
                for c in range(DC):
                    mm = pe.matmul(vp[u][:, 0:D], xct[:, u, 1, c], wv[:, c], start=(c == 0), stop=(c == DC - 1))
                mm.then_inc(v_made, 1)

            turn_tile(0, 0, 0)
            for j in rounds(pe, 0, T // 2 - 1):
                turn_tile(j, j * 2 + 1, 1)
                products(j * 2, 0)
                turn_tile(j + 1, j * 2 + 2, 0)
                products(j * 2 + 1, 1)
            turn_tile(T // 2 - 1, T - 1, 1)
            products(T - 2, 0)
            products(T - 1, 1)

        @block.scalar
        def _(act):
            def keep_turned(t, u):
                act.wait_ge(turned, t + 1)
                act.copy(xct[:, u], turn[u][:, :].rearrange("p (w c n) -> p w c n", w=2, c=DC)).then_inc(xt_ready, 1)

            keep_turned(0, 0)
            keep_turned(1, 1)
            for j in rounds(act, 1, T // 2):
                for u in range(2):
                    t = j * 2 + u
                    act.wait_ge(v_made, t - 1)
                    keep_turned(t, u)

        @block.gpsimd
        def _(pool):
            for t in rounds(pool, 0, T):
                pool.wait_ge(xn_ready, t + 1)
                pool.tensor_tensor(tile(m.x, t), tile(m.x, t), bo, ALU.add).then_inc(biased, 1)
            pool.wait_ge(biased, T)
            pool.wait_ge(var_ready, 1)
            pool.tensor_tensor(m.rstd[:], m.tmp[:, 3], m.c("neg_half"), ALU.pow).then_inc(m.rms_ready, 1)


def attention_phase(m, a):
    nc, sem = m.nc, m.sem
    qn_ready, qk_turned, qkt_kept, k_wide = sem("qn_ready"), sem("qk_turned"), sem("qkt_kept"), sem("k_wide")
    scored, shifted, exped = sem("s_scored"), sem("s_shifted"), sem("s_exped")
    p_turned, pt_kept, v_staged, pv_made = sem("p_turned"), sem("pt_kept"), sem("v_staged"), sem("pv_made")
    pv_kept, pv_turned, o_ready, o_turned, ot_kept = (sem("pv_kept"), sem("pv_turned"), sem("o_ready"),
                                                      sem("o_turned"), sem("ot_kept"))
    wo_made, x_added, padded = sem("wo_made"), sem("x_added"), sem("v_padded")
    var_ready = sem("ln3_var_ready")
    m.ln3_rstd_ready = m.lasting("ln3_rstd_ready")
    G, HG, HH = 4, H // 4, H // DC
    VC = 32

    s = m.stage
    qn = s[:, 0:1024].rearrange("p (u n) -> p u n", u=2)
    qt = s[:, 1024:1536].rearrange("p (u c n) -> p u c n", u=2, c=DC)
    kt = s[:, 1536:2048].rearrange("p (u c n) -> p u c n", u=2, c=DC)
    vs = s[:, 2048:3072].rearrange("p (u h d) -> p u h d", u=2, h=H)
    pvs = s[:, 3072:3584]
    o = s[:, 3584:3840]
    ot = s[:, 3840:4096].rearrange("p (c n) -> p c n", c=DC)
    top, inv = s[:, 4096:4096 + H], s[:, 4112:4112 + H]
    w = m.weights[:, 16384:24576]
    kw = w[:, 0:2048].rearrange("p (c h n) -> p c h n", c=DC, h=HH)
    prob = w[:, 2048:4096]
    pt = w[:, 4096:6144].rearrange("p (g n) -> p g n", g=G)
    qk = m.rows[:, 0:8192].rearrange("p (t n) -> p t n", t=T)
    v = m.rows[:, 8192:12288].rearrange("p (t n) -> p t n", t=T)
    wo = m.proj[:, 1536:2048].rearrange("p (c n) -> p c n", c=DC)
    gq, gk = m.bias[:, 2 * D:3 * D], m.bias[:, 3 * D:4 * D]
    scores = m.psum[:, 0:G].rearrange("p g n -> p (g n)").rearrange("p (c h n) -> p c h n", c=DC, h=HH)
    pt_ps, qk_ps, pv_ps, o_ps = m.ps[4:6], m.ps[6], m.ps[6], m.ps[7]
    pv = o_ps.rearrange("p (h d) -> p h d", h=H)
    ident = m.c("ident")

    with nc.Block() as block:

        @block.vector
        def _(dve):
            steps = m.dve_steps(dve)
            dve.wait_ge(m.rms_ready, 1)

            def norm_qk(t, u):
                if not isinstance(t, int) or t >= 2:
                    dve.wait_ge(qk_turned, t - 1)
                dve.scalar_tensor_tensor(qn[:, u, 0:D], tile(qk, t)[:, 0:D], col(m.rstd[:, 0:T], t), gq, ALU.mult, ALU.mult)
                dve.scalar_tensor_tensor(qn[:, u, D:2 * D], tile(qk, t)[:, D:2 * D], col(m.rstd[:, T:2 * T], t), gk,
                                         ALU.mult, ALU.mult).then_inc(qn_ready, 1)

            def find_top(t, c):
                dve.wait_ge(scored, t * 2 + (c + 1))
                return steps.did(dve.tensor_reduce(top[:, c * HH:(c + 1) * HH], scores[:, c], X_AXIS, ALU.max))

            def shift(t, c, top_at):
                steps.wait(top_at)
                if not isinstance(t, int) or t >= 1:
                    dve.wait_ge(p_turned, t * G - (2 - 2 * c))
                dve.tensor_tensor(prob[:, c * 1024:(c + 1) * 1024].rearrange("p (h n) -> p h n", h=HH), scores[:, c],
                                  top[:, c * HH:(c + 1) * HH].unsqueeze(2).to_broadcast([P, HH, S]),
                                  ALU.subtract).then_inc(shifted, 1)

            def normed_out(t):
                dve.wait_ge(pv_turned, t + 1)
                steps.did(dve.reciprocal(inv.unsqueeze(2), pv[:, :, HD:HD + 1]))
                steps.wait()
                if not isinstance(t, int) or t >= 1:
                    dve.wait_ge(o_turned, t)
                dve.tensor_tensor(o.rearrange("p (h d) -> p h d", h=H), pv[:, :, 0:HD],
                                  inv.unsqueeze(2).to_broadcast([P, H, HD]), ALU.mult).then_inc(o_ready, 1)

            def add(t):
                dve.wait_ge(wo_made, t + 1)
                dve.tensor_tensor(tile(m.x, t), tile(m.x, t), o_ps[:, D:2 * D], ALU.add).then_inc(x_added, 1)

            def stats(t):
                dve.wait_ge(x_added, t + 1)
                steps.did(dve.bn_stats(tile(m.stats[:, 0], t), tile(m.x, t)))

            def step(t, u, before=True, after=2):
                if after >= 2:
                    norm_qk(t + 2, u)
                if after:
                    n = find_top(t + 1, 0)
                if before:
                    normed_out(t - 1)
                if after:
                    shift(t + 1, 0, n)
                    n = find_top(t + 1, 1)
                    shift(t + 1, 1, n)
                if before:
                    add(t - 1)
                    stats(t - 1)

            norm_qk(0, 0)
            norm_qk(1, 1)
            for c in range(DC):
                shift(0, c, find_top(0, c))
            step(0, 0, before=False)
            step(1, 1)
            base = steps.n
            with dve.Fori(1, T // 2 - 1) as j:
                for u in range(2):
                    steps.n = base + (j - 1) * 8 + 4 * u
                    step(j * 2 + u, u)
            steps.n = base + (T // 2 - 2) * 8
            step(T - 2, 0, after=1)
            step(T - 1, 1, after=0)
            normed_out(T - 1)
            add(T - 1)
            stats(T - 1)
            steps.wait()
            finish_stats(m, dve, steps, m.stats[:, 0], m.mean[:], m.tmp[:, 3, 0:T], LN_EPS, T).then_inc(var_ready, 1)

        @block.tensor
        def _(pe):
            def turn_qk(t, u):
                pe.wait_ge(qn_ready, t + 1)
                for i in range(4):
                    mm = pe.transpose(qk_ps[:, i * P:(i + 1) * P], qn[:, u, i * P:(i + 1) * P], ident)
                mm.then_inc(qk_turned, 1)

            def score(t, u):
                for c in range(DC):
                    pe.wait_ge(k_wide, t * 2 + (c + 1))
                    if not isinstance(t, int) or t >= 1:
                        pe.wait_ge(shifted, t * 2 + (c - 1))
                    for g in range(2):
                        mm = pe.matmul(m.ps[c * 2 + g], qt[:, u, c],
                                       kw[:, c, g * HG:(g + 1) * HG].rearrange("p h n -> p (h n)"), start=True, stop=True)
                    mm.then_inc(scored, 1)

            def turn_probs(t, g):
                pe.wait_ge(exped, t * 2 + (g // 2 + 1))
                if g >= 2 or not isinstance(t, int) or t >= 1:
                    pe.wait_ge(pt_kept, t * G + (g - 1))
                for i in range(HG):
                    at = g * HG + i
                    mm = pe.transpose(pt_ps[g % 2][:, i * P:(i + 1) * P], prob[:, at * P:(at + 1) * P], ident)
                mm.then_inc(p_turned, 1)

            def values(t, u, g, j):
                pe.wait_ge(pt_kept, t * G + (g + 1))
                if g == 0:
                    pe.wait_ge(v_staged, t + 1)
                for i in range(HG):
                    mm = pe.matmul(pv_ps[VC * i:VC * (i + 1), g * P:(g + 1) * P], vs[:, u, g * HG + i],
                                   pt[:, g, i * P:(i + 1) * P], start=True, stop=True)
                mm.then_inc(pv_made, 1)

            def turn_back(t):
                pe.wait_ge(pv_kept, t + 1)
                if not isinstance(t, int) or t >= 1:
                    pe.wait_ge(x_added, t)
                for g in range(G):
                    mm = pe.transpose(o_ps[:, g * P:(g + 1) * P], pvs[:, g * P:(g + 1) * P], ident)
                mm.then_inc(pv_turned, 1)

            def turn_out(t):
                pe.wait_ge(o_ready, t + 1)
                for c in range(DC):
                    mm = pe.transpose(o_ps[:, c * P:(c + 1) * P], o[:, c * P:(c + 1) * P], ident)
                mm.then_inc(o_turned, 1)

            def project(t):
                pe.wait_ge(ot_kept, t + 1)
                for c in range(DC):
                    mm = pe.matmul(o_ps[:, D:2 * D], ot[:, c], wo[:, c], start=(c == 0), stop=(c == DC - 1))
                mm.then_inc(wo_made, 1)

            def step(t, u, j, before=True, after=2):
                if after:
                    score(t + 1, 1 - u)
                if before:
                    turn_back(t - 1)
                if after >= 2:
                    turn_qk(t + 2, u)
                turn_probs(t, 0)
                turn_probs(t, 1)
                if before:
                    turn_out(t - 1)
                if after >= 2:
                    pe.wait_ge(qkt_kept, t + 3)
                values(t, u, 0, j)
                turn_probs(t, 2)
                values(t, u, 1, j)
                turn_probs(t, 3)
                values(t, u, 2, j)
                if before:
                    project(t - 1)
                values(t, u, 3, j)

            turn_qk(0, 0)
            score(0, 0)
            turn_qk(1, 1)
            step(0, 0, 0, before=False)
            step(1, 1, 0)
            with pe.Fori(1, T // 2 - 1) as j:
                for u in range(2):
                    step(j * 2 + u, u, j)
            step(T - 2, 0, T // 2 - 1, after=1)
            step(T - 1, 1, T // 2 - 1, after=0)
            turn_back(T - 1)
            turn_out(T - 1)
            project(T - 1)

        @block.scalar
        def _(act):
            def keep_qk(t, u):
                act.wait_ge(qk_turned, t + 1)
                if not isinstance(t, int) or t >= 2:
                    act.wait_ge(scored, t * 2 - 2)
                    act.wait_ge(k_wide, t * 2 - 2)
                act.copy(qt[:, u], qk_ps[:, 0:D].rearrange("p (c n) -> p c n", c=DC))
                act.copy(kt[:, u], qk_ps[:, D:2 * D].rearrange("p (c n) -> p c n", c=DC)).then_inc(qkt_kept, 1)

            def exp(t, c):
                act.wait_ge(shifted, t * 2 + (c + 1))
                half = prob[:, c * 1024:(c + 1) * 1024]
                act.activation(half, half, ACT.Exp, scale=float(HD) ** -0.5).then_inc(exped, 1)

            def keep_pt(t, g):
                act.wait_ge(p_turned, t * G + (g + 1))
                if not isinstance(t, int) or t >= 1:
                    act.wait_ge(pv_made, t * G - (3 - g))
                act.copy(pt[:, g], pt_ps[g % 2]).then_inc(pt_kept, 1)

            def keep_pv(t):
                act.wait_ge(pv_made, t * G + G)
                if not isinstance(t, int) or t >= 1:
                    act.wait_ge(pv_turned, t)
                act.copy(pvs, pv_ps).then_inc(pv_kept, 1)

            def keep_out(t):
                act.wait_ge(o_turned, t + 1)
                if not isinstance(t, int) or t >= 1:
                    act.wait_ge(wo_made, t)
                act.copy(ot, o_ps[:, 0:D].rearrange("p (c n) -> p c n", c=DC)).then_inc(ot_kept, 1)

            def step(t, u, before=True, after=2):
                if before:
                    keep_pv(t - 1)
                if after >= 2:
                    keep_qk(t + 2, u)
                keep_pt(t, 0)
                keep_pt(t, 1)
                if before:
                    keep_out(t - 1)
                keep_pt(t, 2)
                keep_pt(t, 3)
                if after:
                    exp(t + 1, 0)
                    exp(t + 1, 1)

            keep_qk(0, 0)
            keep_qk(1, 1)
            exp(0, 0)
            exp(0, 1)
            step(0, 0, before=False)
            step(1, 1)
            with act.Fori(1, T // 2 - 1) as j:
                for u in range(2):
                    step(j * 2 + u, u)
            step(T - 2, 0, after=1)
            step(T - 1, 1, after=0)
            keep_pv(T - 1)
            keep_out(T - 1)

        @block.gpsimd
        def _(pool):
            pool.memset(vs[:, :, :, :], 0.0).then_inc(padded, 1)
            pool.wait_ge(padded, 1)
            pool.memset(vs[:, :, :, HD:HD + 1], 1.0).then_inc(padded, 1)
            pool.wait_ge(padded, 2)
            heads = m.c("heads").unsqueeze(2).to_broadcast([P, HH, S])

            def widen(t, u):
                pool.wait_ge(qkt_kept, t + 1)
                for c in range(DC):
                    if not isinstance(t, int) or t >= 1:
                        pool.wait_ge(scored, t * 2 - (1 - c))
                    pool.tensor_tensor(kw[:, c], kt[:, u, c].unsqueeze(1).to_broadcast([P, HH, S]), heads,
                                       ALU.mult).then_inc(k_wide, 1)

            def stage_v(t, u):
                if not isinstance(t, int) or t >= 2:
                    pool.wait_ge(pv_made, t * G - G)
                pool.tensor_copy(vs[:, u, :, 0:HD], tile(v, t).rearrange("p (h d) -> p h d", h=H)).then_inc(v_staged, 1)

            for j in rounds(pool, 0, T // 2):
                for u in range(2):
                    widen(j * 2 + u, u)
                    stage_v(j * 2 + u, u)
            pool.wait_ge(var_ready, 1)
            pool.tensor_tensor(m.rstd[:, 0:T], m.tmp[:, 3, 0:T], m.c("neg_half")[:, 0:T], ALU.pow).then_inc(m.ln3_rstd_ready, 1)


def experts1_phase(m, a):
    nc, sem = m.nc, m.sem
    NB, BUFS = NB1, 4
    PAIRS = NB // 2
    LIMIT, ALPHA = 7.0, 1.702
    rows_in = [sem(f"e1_in{i}") for i in range(BUFS)]
    stored = [sem(f"e1_stored{i}") for i in range(BUFS)]
    taken = [sem(f"e1_taken{i}") for i in range(BUFS)]
    out_ready = [sem(f"e1_out{i}") for i in range(BUFS)]
    bias_in, bias_split, bias_rows = sem("e1_bias_in"), sem("e1_bias_split"), sem("e1_bias_rows")
    bias_out, zeroed = sem("e1_bias_out"), sem("e1_zeroed")
    turned, xt_ready, gu_made = sem("e1_turned"), sem("e1_xt_ready"), sem("e1_gu_made")
    gate_ready, sig_ready, h_ready = sem("e1_gate_ready"), sem("e1_sig_ready"), sem("e1_h_ready")
    h_turned, ht_ready, down_made, y_kept = sem("e1_h_turned"), sem("e1_ht_ready"), sem("e1_down_made"), sem("e1_y_kept")
    ones_ready = sem("e1_ones_ready")

    r, s = m.rows, m.stage
    gub = r[:, 0:4096].bitcast(BF16)
    db = r[:, 4096:6144].bitcast(BF16)
    xg = r[:, 6144:7168].rearrange("p (i n) -> p i n", i=BUFS)
    yo = r[:, 7168:8192].rearrange("p (i n) -> p i n", i=BUFS)
    gate, up, sig, upg = (r[:, at:at + 1024].rearrange("p (u w n) -> p u w n", u=2, w=2)
                          for at in (8192, 9216, 10240, 11264))
    ones3 = r[:, 12288:12352].bitcast(BF16)
    raw, rest = s[:, 3072:3168], s[:, 3168:3264]
    split = s[:, 3264:3408].bitcast(BF16).rearrange("p (i n) -> p i n", i=3)
    hid = s[:, 0:1024].rearrange("p (u w n) -> p u w n", u=2, w=2)
    xt = s[:, 1024:2048].rearrange("p (u w c n) -> p u w c n", u=2, w=2, c=DC)
    ht = s[:, 2048:3072].rearrange("p (u w c n) -> p u w c n", u=2, w=2, c=DC)
    gu = [m.psum[:, 2 * u:2 * u + 2] for u in range(2)]
    x_turn, h_turn, y_ps = m.ps[4], m.ps[5], m.ps[6]
    ident = m.c("ident")
    wgu = m.weights[:, 0:16384].rearrange("p (e c f) -> p e c f", e=E1, c=DC)
    wd = m.weights[:, 16384:24576].rearrange("p (e c n) -> p e c n", e=E1, c=DC)

    with nc.Block() as block:

        @block.sync
        def _(sp):
            sp.dma_start(raw[:, 0:64], a["L1_ffn_gate_up_proj_bias"].rearrange("e f -> (e f)").rearrange("(p n) -> p n", p=P)).then_inc(bias_in, 16)
            sp.dma_start(raw[:, 64:96], a["L1_ffn_down_proj_bias"].rearrange("e f -> (e f)").rearrange("(p n) -> p n", p=P)).then_inc(bias_in, 16)
            gu_parts, d_parts = a["bias_parts"][:, 0:E1 * 2 * F1], a["bias_parts"][:, E1 * 2 * F1:]
            sp.wait_ge(bias_split, 3)
            sp.dma_start(gu_parts.rearrange("i (p n) -> p i n", p=P), split[:, :, 0:64]).then_inc(bias_out, 16)
            sp.dma_start(d_parts.rearrange("i (p n) -> p i n", p=P), split[:, :, 64:96]).then_inc(bias_out, 16)
            sp.wait_ge(bias_out, 32)
            sp.wait_ge(zeroed, 1)
            sp.dma_start(gub[0:3], gu_parts).then_inc(bias_rows, 16)
            sp.dma_start(db[0:3], d_parts).then_inc(bias_rows, 16)

        @block.gpsimd
        def _(pool):
            pool.memset(r[:, 0:6144], 0.0).then_inc(zeroed, 1)
            gather_and_scatter(m, pool, a, 1, xg, rows_in, taken, yo, out_ready, stored, NB, BUFS, 8)

        @block.vector
        def _(dve):
            steps = m.dve_steps(dve)
            dve.memset(ones3, 1.0).then_inc(ones_ready, 1)
            dve.wait_ge(bias_in, 32)
            left = raw
            for i in range(3):
                dve.tensor_copy(split[:, i], left).then_inc(bias_split, 1)
                if i < 2:
                    dve.wait_ge(bias_split, i + 1)
                    steps.did(dve.tensor_tensor(rest, left, split[:, i], ALU.subtract))
                    steps.wait()
                    left = rest
            base = steps.n
            for j in rounds(dve, 0, PAIRS // 2):
                steps.n = base + j * 4
                for u in range(2):
                    p = j * 2 + u
                    dve.wait_ge(gu_made, p + 1)
                    dve.tensor_scalar(gate[:, u], gu[u][:, :, 0:F1], LIMIT, None, ALU.min).then_inc(gate_ready, 1)
                    steps.did(dve.tensor_scalar(up[:, u], gu[u][:, :, F1:2 * F1], LIMIT, -LIMIT, ALU.min, ALU.max))
                    dve.wait_ge(sig_ready, p + 1)
                    steps.wait()
                    steps.did(dve.scalar_tensor_tensor(upg[:, u], up[:, u], 1.0, sig[:, u], ALU.add, ALU.mult))
                    steps.wait()
                    dve.wait_ge(h_turned, p)
                    dve.tensor_tensor(hid[:, u], upg[:, u], gate[:, u], ALU.mult).then_inc(h_ready, 1)

        @block.tensor
        def _(pe):
            def turn_rows(j, p, u):
                pe.wait_ge(xt_ready, p)
                for w in range(2):
                    i = 2 * u + w
                    pe.wait_ge(rows_in[i], j * 16 + 16)
                    for c in range(DC):
                        at = (w * DC + c) * P
                        mm = pe.transpose(x_turn[:, at:at + P], xg[:, i, c * P:(c + 1) * P], ident)
                    mm.then_inc(taken[i], 1)

            def gate_up(p, experts, u):
                pe.wait_ge(xt_ready, p + 1)
                if not isinstance(p, int) or p >= 2:
                    pe.wait_ge(h_ready, p - 1)
                for w, e in enumerate(experts):
                    pe.matmul(gu[u][:, w], ones3, gub[:, bass.ds(e * 2 * F1, 2 * F1)], start=True, stop=False)
                    for c in range(DC):
                        rhs = wgu[:, bass.ds(e, 1), c].rearrange("p a f -> p (a f)")
                        mm = pe.matmul(gu[u][:, w], xt[:, u, w, c], rhs, start=False, stop=(c == DC - 1))
                mm.then_inc(gu_made, 1)

            def turn_hidden(p, u):
                pe.wait_ge(h_ready, p + 1)
                pe.wait_ge(ht_ready, p)
                for w in range(2):
                    for c in range(DC):
                        at = (w * DC + c) * P
                        mm = pe.transpose(h_turn[:, at:at + P], hid[:, u, w, c * P:(c + 1) * P], ident)
                mm.then_inc(h_turned, 1)

            def down(p, experts, u):
                pe.wait_ge(ht_ready, p + 1)
                pe.wait_ge(y_kept, p)
                for w, e in enumerate(experts):
                    out = y_ps[:, w * D:(w + 1) * D]
                    pe.matmul(out, ones3, db[:, bass.ds(e * D, D)], start=True, stop=False)
                    for c in range(DC):
                        rhs = wd[:, bass.ds(e, 1), c].rearrange("p a n -> p (a n)")
                        mm = pe.matmul(out, ht[:, u, w, c], rhs, start=False, stop=(c == DC - 1))
                mm.then_inc(down_made, 1)

            def experts(p):
                return [pe.value_load(m.block_expert[0:1, bass.ds(p * 2 + w, 1)], min_val=0, max_val=E1 - 1) for w in range(2)]

            def step(j, u, last=False):
                p = j * 2 + u
                e, e_before = experts(p), experts(p - 2)
                turn_hidden(p - 2, u)
                gate_up(p, e, u)
                if not last:
                    turn_rows(j + u, p + 1, 1 - u)
                down(p - 2, e_before, u)

            pe.wait_ge(m.w1_in, 16 * 2 * E1)
            pe.wait_ge(ones_ready, 1)
            pe.wait_ge(bias_rows, 32)
            turn_rows(0, 0, 0)
            gate_up(0, experts(0), 0)
            turn_rows(0, 1, 1)
            gate_up(1, experts(1), 1)
            turn_rows(1, 2, 0)
            for j in rounds(pe, 1, PAIRS // 2 - 1):
                step(j, 0)
                step(j, 1)
            step(PAIRS // 2 - 1, 0)
            step(PAIRS // 2 - 1, 1, last=True)
            for u in range(2):
                p = PAIRS - 2 + u
                turn_hidden(p, u)
                down(p, experts(p), u)

        @block.scalar
        def _(act):
            def keep_rows(p, u):
                act.wait_ge(taken[2 * u + 1], p // 2 + 1 if isinstance(p, int) else p)
                act.copy(xt[:, u], x_turn[:, :].rearrange("p (w c n) -> p w c n", w=2, c=DC)).then_inc(xt_ready, 1)

            def sigmoid(p, u):
                act.wait_ge(gate_ready, p + 1)
                act.activation(sig[:, u], gate[:, u], ACT.Sigmoid, scale=ALPHA).then_inc(sig_ready, 1)

            def keep_hidden(p, u):
                act.wait_ge(h_turned, p + 1)
                act.copy(ht[:, u], h_turn[:, :].rearrange("p (w c n) -> p w c n", w=2, c=DC)).then_inc(ht_ready, 1)

            def keep_out(j, p, u):
                act.wait_ge(down_made, p + 1)
                for w in range(2):
                    i = 2 * u + w
                    act.wait_ge(stored[i], j * 16)
                    ins = act.copy(yo[:, i], y_ps[:, w * D:(w + 1) * D])
                    ins.then_inc(out_ready[i], 1)
                    act.wait_ge(out_ready[i], j + 1)
                act.sem_inc(y_kept, 1)

            def step(j, u, last=False):
                p = j * 2 + u
                keep_hidden(p - 2, u)
                sigmoid(p, u)
                if not last:
                    act.wait_ge(taken[2 * (1 - u) + 1], j + u + 1)
                    act.copy(xt[:, 1 - u], x_turn[:, :].rearrange("p (w c n) -> p w c n", w=2, c=DC)).then_inc(xt_ready, 1)
                keep_out(j - 1, p - 2, u)

            keep_rows(0, 0)
            keep_rows(1, 1)
            sigmoid(0, 0)
            act.wait_ge(taken[1], 2)
            act.wait_ge(gu_made, 1)
            act.copy(xt[:, 0], x_turn[:, :].rearrange("p (w c n) -> p w c n", w=2, c=DC)).then_inc(xt_ready, 1)
            sigmoid(1, 1)
            for j in rounds(act, 1, PAIRS // 2 - 1):
                step(j, 0)
                step(j, 1)
            step(PAIRS // 2 - 1, 0)
            step(PAIRS // 2 - 1, 1, last=True)
            for u in range(2):
                keep_hidden(PAIRS - 2 + u, u)
                keep_out(PAIRS // 2 - 1, PAIRS - 2 + u, u)


SCRATCH = [("xn0", TOKENS), ("y0", TOKENS * K0 + P * NB0), ("xn1", TOKENS), ("y1", TOKENS * K1 + P * NB1)]


def first_experts(m, a):
    logits_phase(m, a, 0)
    routing_phase(m, a, 0)
    experts0_phase(m, a)
    combine_phase(m, a, 0)
    m.recycle()


def second_experts(m, a):
    logits_phase(m, a, 1)
    routing_phase(m, a, 1)
    experts1_phase(m, a)
    combine_phase(m, a, 1)


PHASES = [context_phase, retention_scores_phase, retention_output_phase, retention_close_phase,
          first_experts, projections_phase, attention_phase, second_experts]


def build(nc, a, phases=None):
    with ExitStack() as ctx:
        m = Memory(nc, ctx)
        m.w0_in = m.lasting("w0_in")
        m.dve_chain = m.lasting("dve_chain")
        m.all_steps = {}
        m.act_table = None

        def dve_steps(eng):
            if "dve" not in m.all_steps:
                m.all_steps["dve"] = Steps(eng, m.dve_chain)
            m.all_steps["dve"].eng = eng
            return m.all_steps["dve"]

        m.dve_steps = dve_steps
        wg = m.weights[:, 0:8192].rearrange("p (e c f) -> p e c f", e=E0, c=DC)
        wu = m.weights[:, 8192:16384].rearrange("p (e c f) -> p e c f", e=E0, c=DC)
        wd = m.weights[:, 16384:24576].rearrange("p (e c n) -> p e c n", e=E0, c=F0 // P)
        m.wg0, m.wu0, m.wd0 = (lambda e: wg[:, e]), (lambda e: wu[:, e]), (lambda e: wd[:, e])
        for phase in PHASES[:phases]:
            phase(m, a)


def constants():
    import numpy as np
    c = {}
    i = np.arange(P)
    c["ident"] = np.eye(P)
    c["before"] = (i[:, None] < i[None, :])
    c["ones"] = np.ones((P, P))
    c["iota"] = np.tile(i, (P, 1))
    g = (1.0 - 2.0 ** (-5.0 - np.arange(RH, dtype=np.float64)))
    expo = i[None, :] - i[:, None]
    dm = np.where(expo[None] <= 0, g[:, None, None] ** expo[None].astype(np.float64), 0.0)
    dn = dm / np.sqrt(dm.sum(-1))[:, None, :] / np.sqrt(float(RHD))
    c["decay"] = dn.transpose(1, 0, 2).reshape(P, -1)
    et = np.zeros((E1, T))
    c["expert"] = np.tile((et + np.arange(E1)[:, None]).reshape(1, -1), (P, 1))
    c["carry"] = np.tile((et + (np.arange(T) > 0)).reshape(1, -1), (P, 1))
    c["full"] = np.tile((et + P * np.arange(T)).reshape(1, -1), (P, 1))
    token = i[:, None] + P * np.arange(T)[None, :]
    c["dest0"] = token + 1
    c["dest1"] = (token[:, None, :] * K1 + np.arange(K1)[None, :, None] + 1).reshape(P, -1)
    c["trash0"] = TOKENS * K0 + 1 + P * np.arange(NB0)[None, :] + i[:, None]
    c["trash1"] = TOKENS * K1 + 1 + P * np.arange(NB1)[None, :] + i[:, None]
    c["heads"] = i[:, None] // HD == np.arange(H // 2)[None, :]
    c["neg_half"] = np.full((P, 2 * T), -0.5)
    return np.ascontiguousarray(np.concatenate([c[n] for n, _ in CONST_PARTS], axis=1).astype(np.float32))


_SKIP = ("L1_xattn_context_lens", "L1_xattn_Wk", "L1_xattn_bk", "L1_xattn_gk", "L1_xattn_Wv", "L1_xattn_bv",
         "L1_ffn_router_weight")


def layout(inputs):
    import numpy as np
    arrays = {}
    for name, v in inputs.items():
        if name in _SKIP:
            continue
        arrays[name] = np.ascontiguousarray(v)
    arrays["x"] = arrays["x"].reshape(TOKENS, D)
    arrays["ctx_2048"] = arrays["ctx_2048"].reshape(TOKENS, D)
    gu = arrays["L1_ffn_gate_up_proj"].reshape(E1, D, F1, 2)
    arrays["L1_ffn_gate_up_proj"] = np.ascontiguousarray(gu.transpose(0, 1, 3, 2)).reshape(E1, D, 2 * F1)
    gb = arrays["L1_ffn_gate_up_proj_bias"].reshape(E1, F1, 2)
    arrays["L1_ffn_gate_up_proj_bias"] = np.ascontiguousarray(gb.transpose(0, 2, 1)).reshape(E1, 2 * F1)
    arrays["router1"] = np.ascontiguousarray(np.asarray(inputs["L1_ffn_router_weight"]).T)
    arrays["const"] = constants()
    return arrays


def kernel(**inputs):
    import concourse.bacc as bacc
    from concourse.bass_utils import run_bass_kernel_spmd

    nc = bacc.Bacc("TRN2", target_bir_lowering=False, num_devices=1)
    arrays = layout(inputs)
    a = {n: nc.dram_tensor(f"in_{n}", v.shape, mybir.dt.from_np(v.dtype), kind="ExternalInput").ap()
         for n, v in arrays.items()}
    a["out"] = nc.dram_tensor("out", (TOKENS, D), F32, kind="ExternalOutput").ap()
    for name, rows in SCRATCH:
        a[name] = nc.dram_tensor(name, (rows, D), F32, kind="Internal").ap()
    a["bias_parts"] = nc.dram_tensor("bias_parts", (3, E1 * (2 * F1 + D)), BF16, kind="Internal").ap()
    build(nc, a)
    r = run_bass_kernel_spmd(nc, [{f"in_{n}": v for n, v in arrays.items()}], core_ids=[0])
    return r.results[0]["out"].reshape(B, S, D)
```
